# Optimizing a Trainium2 kernel written in Bass

```python
import numpy as np
import jax
import jax.numpy as jnp

def _softmax(x, axis=-1):
    return jax.nn.softmax(x, axis=axis)

def _gelu(x):
    return jax.nn.gelu(x, approximate=True)

def _silu(x):
    return jax.nn.silu(x)

def _sigmoid(x):
    return jax.nn.sigmoid(x)

def _layernorm(x, axis=-1, eps=1e-05):
    m = jnp.mean(x, axis=axis, keepdims=True)
    v = jnp.var(x, axis=axis, keepdims=True)
    return (x - m) / jnp.sqrt(v + eps)

def _scatter_add(tgt, idx, src, axis=0):
    return tgt.at[idx].add(src)

def _segment_sum(src, seg, n):
    return jax.ops.segment_sum(src, seg, n)
kernel_name = 'mk_gnn_preln_d1_gnn_r64_d72bfb'

def setup_inputs(seed: int=0):
    np.random.seed(seed)
    _w = jnp.asarray

    def _rec_inputs():
        import jax
        import jax.numpy as jnp
        _gk = jax.random.key(seed)
        x = -0.000202 + 1 * jax.random.normal(jax.random.fold_in(_gk, 1), (50000, 128), jnp.float32)
        src = jax.random.randint(jax.random.fold_in(_gk, 2), (12500,), 0, 50000, jnp.int32)
        dst = jax.random.randint(jax.random.fold_in(_gk, 3), (12500,), 0, 50000, jnp.int32)
        _o = jnp.argsort(dst, stable=True)
        src = src[_o]
        dst = dst[_o]
        edge_attr_128 = 4.59472e-05 + 1.00006 * jax.random.normal(jax.random.fold_in(_gk, 11), (12500, 128), jnp.float32)
        return (x, src, dst, edge_attr_128)
    x, src, dst, edge_attr_128 = _rec_inputs()

    def _L0_gnn_setup():
        import jax, jax.numpy as jnp
        import numpy as np
        N = 50000
        E = 625000
        D = 128
        DF = 4 * D

        def layernorm(x, gamma, beta, eps=1e-05):
            mu = jnp.mean(x, axis=-1, keepdims=True)
            var = jnp.var(x, axis=-1, keepdims=True)
            return (x - mu) * jax.lax.rsqrt(var + eps) * gamma + beta
        key = jax.random.key(seed)
        ks = jax.random.split(key, 12)
        s = 1.0 / np.sqrt(D)
        sf = 1.0 / np.sqrt(DF)
        return {'x': jax.random.normal(ks[0], (N, D), jnp.float32), 'edge_index': jax.random.randint(ks[1], (2, E), 0, N, jnp.int32), 'edge_attr': jax.random.normal(ks[2], (E, D), jnp.float32), 'g1': jnp.ones((D,), jnp.float32), 'b1': jnp.zeros((D,), jnp.float32), 'g2': jnp.ones((D,), jnp.float32), 'b2': jnp.zeros((D,), jnp.float32), 'eps_gin': jnp.zeros((), jnp.float32), 'Wg1': jax.random.uniform(ks[3], (D, D), jnp.float32, -s, s), 'bg1': jnp.zeros((D,), jnp.float32), 'Wg2': jax.random.uniform(ks[4], (D, D), jnp.float32, -s, s), 'bg2': jnp.zeros((D,), jnp.float32), 'Wf1': jax.random.uniform(ks[5], (D, DF), jnp.float32, -s, s), 'bf1': jnp.zeros((DF,), jnp.float32), 'Wf2': jax.random.uniform(ks[6], (DF, D), jnp.float32, -sf, sf), 'bf2': jnp.zeros((D,), jnp.float32)}
    _L0_gnn_all = _L0_gnn_setup()
    _L0_gnn_in = {k: v for k, v in _L0_gnn_all.items() if k in ('g1', 'b1', 'g2', 'b2', 'eps_gin', 'Wg1', 'bg1', 'Wg2', 'bg2', 'Wf1', 'bf1', 'Wf2', 'bf2')}
    del _L0_gnn_all
    return {'x': x, 'src': src, 'dst': dst, 'edge_attr_128': edge_attr_128, 'L0_gnn_g1': _L0_gnn_in['g1'], 'L0_gnn_b1': _L0_gnn_in['b1'], 'L0_gnn_g2': _L0_gnn_in['g2'], 'L0_gnn_b2': _L0_gnn_in['b2'], 'L0_gnn_eps_gin': _L0_gnn_in['eps_gin'], 'L0_gnn_Wg1': _L0_gnn_in['Wg1'], 'L0_gnn_bg1': _L0_gnn_in['bg1'], 'L0_gnn_Wg2': _L0_gnn_in['Wg2'], 'L0_gnn_bg2': _L0_gnn_in['bg2'], 'L0_gnn_Wf1': _L0_gnn_in['Wf1'], 'L0_gnn_bf1': _L0_gnn_in['bf1'], 'L0_gnn_Wf2': _L0_gnn_in['Wf2'], 'L0_gnn_bf2': _L0_gnn_in['bf2']}

def reference(x, src, dst, edge_attr_128, L0_gnn_g1, L0_gnn_b1, L0_gnn_g2, L0_gnn_b2, L0_gnn_eps_gin, L0_gnn_Wg1, L0_gnn_bg1, L0_gnn_Wg2, L0_gnn_bg2, L0_gnn_Wf1, L0_gnn_bf1, L0_gnn_Wf2, L0_gnn_bf2):
    import jax
    import jax.numpy as jnp

    def _L0_gnn_ref(x, edge_index, edge_attr, g1, b1, g2, b2, eps_gin, Wg1, bg1, Wg2, bg2, Wf1, bf1, Wf2, bf2):
        import jax, jax.numpy as jnp
        import numpy as np
        N = 50000
        E = 625000
        D = 128
        DF = 4 * D

        def layernorm(x, gamma, beta, eps=1e-05):
            mu = jnp.mean(x, axis=-1, keepdims=True)
            var = jnp.var(x, axis=-1, keepdims=True)
            return (x - mu) * jax.lax.rsqrt(var + eps) * gamma + beta
        src = edge_index[0]
        dst = edge_index[1]
        xn = layernorm(x, g1, b1)
        msg = jax.nn.relu(xn[src] + edge_attr)
        aggr = jax.ops.segment_sum(msg, dst, num_segments=N)
        h = (1.0 + eps_gin) * xn + aggr
        h = jax.nn.relu(h @ Wg1 + bg1) @ Wg2 + bg2
        x = x + h
        xn2 = layernorm(x, g2, b2)
        f = jax.nn.gelu(xn2 @ Wf1 + bf1, approximate=False) @ Wf2 + bf2
        return x + f
    edge_index = jnp.stack([src, dst])
    h = jnp.maximum(_layernorm(x, axis=-1), 0.0)
    x = x + _L0_gnn_ref(h, edge_index, edge_attr_128, L0_gnn_g1, L0_gnn_b1, L0_gnn_g2, L0_gnn_b2, L0_gnn_eps_gin, L0_gnn_Wg1, L0_gnn_bg1, L0_gnn_Wg2, L0_gnn_bg2, L0_gnn_Wf1, L0_gnn_bf1, L0_gnn_Wf2, L0_gnn_bf2)
    return x

_drawn_inputs = setup_inputs


def setup_inputs(seed=0):
    import zlib

    import numpy as np

    out = dict(_drawn_inputs(seed))
    spreads = {'L0_gnn_g1': (1.0, 0.2),
     'L0_gnn_b1': (0.0, 0.469),
     'L0_gnn_g2': (1.0, 0.6),
     'L0_gnn_b2': (0.0, 0.681),
     'L0_gnn_bg1': (0.0, 0.328),
     'L0_gnn_bg2': (0.0, 0.1),
     'L0_gnn_bf1': (0.0, 0.372),
     'L0_gnn_bf2': (0.0, 0.1)}
    factors = {}
    for name, (base, spread) in spreads.items():
        noise = np.random.default_rng([zlib.crc32(name.encode()), seed]).standard_normal(out[name].shape)
        drawn = base * np.exp(spread * noise) if base else spread * noise
        out[name] = jnp.asarray(drawn.astype(out[name].dtype))
    for name, factor in factors.items():
        out[name] = (out[name] * factor).astype(out[name].dtype)
    return out
```

```python
import concourse.bass as bass
from concourse import mybir
from contextlib import ExitStack

P = 128
TILES = 4
ROWS = P * TILES


class Turn:

    def __init__(self, q, half=0, low=None):
        self.q, self.half, self.low = q, half, q if low is None else low
        self.slot = q % 2

    def done(self, per_turn=1, back=0):
        return self.half * (2 * per_turn) + (self.q - back + 1) * per_turn

    def done_in_slot(self, per_turn=16, back=0):
        assert back % 2 == 0
        return self.half * per_turn + (self.q // 2 - back // 2 + 1) * per_turn

    def after(self, n):
        return Turn(self.q + n, self.half, self.low + n)

    def row(self, total):
        if isinstance(self.half, int):
            return min(self.q * ROWS, total - ROWS)
        return self.half * (2 * ROWS) + self.q * ROWS


def gnn_layer(nc, x, src, dst, edge_attr, g1, b1, g2, b2, eps_gin, Wg1, bg1, Wg2, bg2, Wf1, bf1, Wf2, bf2, out):
    f32, f32r, i32 = mybir.dt.float32, mybir.dt.float32r, mybir.dt.int32
    ALU, ACT = mybir.AluOpType, mybir.ActivationFunctionType

    NODES, D = x.shape
    EDGES = src.shape[0]
    HIDDEN = Wf1.shape[1]
    HC = HIDDEN // P
    LN_EPS = 1e-5
    GROUPS = -(-NODES // ROWS)
    STEPS = -(-EDGES // ROWS)
    LAST_P = (EDGES - (STEPS - 1) * ROWS) // TILES
    FILL = 8
    FILL_PARTS = 5
    TABLE = -(-(NODES + ROWS) // (P * FILL * FILL_PARTS)) * P * FILL * FILL_PARTS
    assert D == P and HIDDEN % P == 0 and (EDGES - (STEPS - 1) * ROWS) % TILES == 0
    assert NODES >= ROWS and GROUPS % 2 == 0 and GROUPS >= 8 and STEPS % 2 == 1 and STEPS >= 7

    table = nc.dram_tensor("aggregate_table", (TABLE, D), f32).ap()

    ctx = ExitStack()
    with ctx:
        def sb(name, shape, dt=f32):
            return ctx.enter_context(nc.sbuf_tensor(name, shape, dt))

        def pb(name, shape):
            return ctx.enter_context(nc.psum_tensor(name, shape, f32))

        def sem(name):
            return ctx.enter_context(nc.semaphore(name))

        def sem2(name):
            return [sem(f"{name}_{k}") for k in range(2)]

        ident = sb("ident", [P, P])
        before = sb("before", [P, P])
        ones_col = sb("ones_col", [P, 1])
        neg_half = sb("neg_half", [P, 2 * TILES])
        dummy_row = sb("dummy_row", [P, TILES])
        g1_rows = sb("g1_rows", [P, P])
        b1_rows = sb("b1_rows", [P, P])
        g1_eps = sb("g1_eps", [P, P])
        bg2_rows = sb("bg2_rows", [P, P])
        bf2_rows = sb("bf2_rows", [P, ROWS])
        b1_tiles = sb("b1_tiles", [P, ROWS])
        fill_rows = sb("fill_rows", [P, FILL * P])
        eps_col = sb("eps_col", [P, 1])
        one_eps = sb("one_eps", [P, 1])
        g2_col = sb("g2_col", [P, 1])
        b2_col = sb("b2_col", [P, 1])
        bg1_col = sb("bg1_col", [P, 1])
        bf1_col = sb("bf1_col", [P, HC])
        bf1_all = sb("bf1_all", [P, HC])
        wg1 = sb("wg1", [P, P])
        wg2 = sb("wg2", [P, P])
        wf1 = sb("wf1", [P, HIDDEN])
        wf1_g = sb("wf1_g", [P, HIDDEN])
        wf1_hi = sb("wf1_hi", [P, HIDDEN], f32r)
        wf1_lo = sb("wf1_lo", [P, HIDDEN], f32r)
        wf2 = sb("wf2", [P, HC, P])

        src_i = [sb(f"src_i{k}", [P, TILES], i32) for k in range(2)]
        dst_i = [sb(f"dst_i{k}", [P, TILES], i32) for k in range(2)]
        dst_row_i = [sb(f"dst_row_i{k}", [P, ROWS], i32) for k in range(2)]
        attr = [sb(f"attr{k}", [P, TILES, P]) for k in range(2)]
        xs = [sb(f"xs{k}", [P, TILES, P]) for k in range(2)]
        us = sb("us", [P, TILES, P])
        ws = sb("ws", [P, TILES, P])
        attr_b = sb("attr_b", [P, TILES, P])
        pre = sb("pre", [P, TILES, P])
        msg = [sb(f"msg{k}", [P, TILES, P]) for k in range(2)]
        e_raw = sb("e_raw", [P, TILES, 6])
        e_raw2 = sb("e_raw2", [P, TILES, 6])
        e_mv = sb("e_mv", [P, TILES, 2])
        e_mv2 = sb("e_mv2", [P, TILES, 2])
        e_neg = sb("e_neg", [P, TILES])
        e_var = sb("e_var", [P, TILES])
        e_arg = sb("e_arg", [P, TILES])
        e_r = sb("e_r", [P, TILES])
        dst_f = sb("dst_f", [P, TILES])
        dst_row = sb("dst_row", [P, TILES, P])
        same = sb("same", [P, TILES, TILES * P])
        same_before = sb("same_before", [P, TILES, P])
        to_dummy = sb("to_dummy", [P, TILES])
        move = sb("move", [P, TILES])
        where_i = [sb(f"where_i{k}", [P, TILES], i32) for k in range(2)]
        sums = [sb(f"sums{k}", [P, TILES, P]) for k in range(2)]

        xn = [sb(f"xn{k}", [P, TILES, P]) for k in range(2)]
        tab = [sb(f"tab{k}", [P, TILES, P]) for k in range(2)]
        u = sb("u", [P, TILES, P])
        w = sb("w", [P, TILES, P])
        z = [sb(f"z{k}", [P, TILES, P]) for k in range(2)]
        hb = [sb(f"hb{k}", [P, TILES, P]) for k in range(2)]
        xb = [sb(f"xb{k}", [P, TILES, P]) for k in range(2)]
        raw1 = sb("raw1", [P, TILES, 6])
        raw2 = sb("raw2", [P, TILES, 6])
        raw3 = sb("raw3", [P, TILES, 6])
        mv1 = sb("mv1", [P, TILES, 2])
        mv2 = sb("mv2", [P, TILES, 2])
        mv3 = sb("mv3", [P, TILES, 2])
        neg1 = sb("neg1", [P, TILES])
        neg3 = sb("neg3", [P, TILES])
        var12 = sb("var12", [P, 2 * TILES])
        r12 = sb("r12", [P, 2 * TILES])
        var3 = sb("var3", [P, TILES])
        r3 = sb("r3", [P, TILES])
        nb3 = sb("nb3", [P, TILES])
        zT = sb("zT", [P, ROWS])
        aT = sb("aT", [P, ROWS])
        x2 = sb("x2", [P, TILES, P])
        xn2 = [sb(f"xn2_{k}", [P, TILES, P]) for k in range(2)]
        res = [sb(f"res{k}", [P, TILES, P]) for k in range(2)]
        xT_hi = sb("xT_hi", [P, ROWS], f32r)
        xT_lo = sb("xT_lo", [P, ROWS], f32r)
        hT = sb("hT", [P, HC, ROWS])
        y = [sb(f"y{k}", [P, TILES, P]) for k in range(2)]

        ps_z = pb("ps_z", [P, ROWS])
        ps_a = pb("ps_a", [P, ROWS])
        ps_g = pb("ps_g", [P, ROWS])
        ps_x = pb("ps_x", [P, ROWS])
        ps_h = [pb(f"ps_h{k}", [P, ROWS]) for k in range(3)]
        ps_y = pb("ps_y", [P, ROWS])
        ps_sum = [ps_z, ps_a]
        ps_cnt = [ps_g, ps_x]

        weights_in, consts_set, ident_ready, prep = sem("weights_in"), sem("consts_set"), sem("ident_ready"), sem("prep")
        b2_ready, bf1_folded, fill_ready, table_filled = sem("b2_ready"), sem("bf1_folded"), sem("fill_ready"), sem("table_filled")
        edge_in, gathered = sem2("edge_in"), sem2("gathered")
        es_raw, es_mv, es_neg, es_u, es_raw2, es_mv2 = (sem(n) for n in ("es_raw", "es_mv", "es_neg", "es_u", "es_raw2", "es_mv2"))
        es_var, es_arg, es_r, es_w, es_attr, es_pre, es_msg = (sem(n) for n in ("es_var", "es_arg", "es_r", "es_w", "es_attr", "es_pre", "es_msg"))
        es_dst, es_same, es_cnt, es_move, es_where, es_sum, es_out = (sem(n) for n in ("es_dst", "es_same", "es_cnt", "es_move", "es_where", "es_sum", "es_out"))
        scattered = sem("scattered")
        x_in, tab_in, stored = sem2("x_in"), sem2("tab_in"), sem2("stored")
        n_raw1, n_mv1, n_neg1, n_u, n_raw2, n_mv2 = (sem(n) for n in ("n_raw1", "n_mv1", "n_neg1", "n_u", "n_raw2", "n_mv2"))
        n_var1, n_var2, n_w, n_r12, n_hb, n_z, n_xb = (sem(n) for n in ("n_var1", "n_var2", "n_w", "n_r12", "n_hb", "n_z", "n_xb"))
        n_psz, n_zT, n_psa, n_aT, n_psg, n_x2 = (sem(n) for n in ("n_psz", "n_zT", "n_psa", "n_aT", "n_psg", "n_x2"))
        n_raw3, n_mv3, n_var3, n_r3, n_nb3, n_xn2, n_res = (sem(n) for n in ("n_raw3", "n_mv3", "n_var3", "n_r3", "n_nb3", "n_xn2", "n_res"))
        n_psx, n_hi, n_lo, n_psh, n_gelu, n_y, n_used = (sem(n) for n in ("n_psx", "n_hi", "n_lo", "n_psh", "n_gelu", "n_y", "n_used"))

        def rows_of(tensor, turn, parts=P):
            start = turn.row(NODES if tensor is not edge_attr else STEPS * ROWS)
            return tensor[bass.ds(start, parts * TILES), :].rearrange("(p j) f -> p j f", j=TILES)

        def every_partition(vector, parts=P):
            return bass.AP(vector.tensor, 0, [[0, parts], [1, vector.shape[0]]])

        def column(vector):
            return vector.rearrange("(p o) -> p o", o=1)

        def edge_turns(eng, first, both, last):
            first(Turn(0), P)
            for s in (0, 1):
                both(Turn(s), P, P)
            with eng.Fori(1, (STEPS - 3) // 2) as half:
                for q in range(2):
                    both(Turn(q, half, 2 + q), P, P)
            for s in range(STEPS - 3, STEPS - 1):
                both(Turn(s), P, P if s + 1 < STEPS - 1 else LAST_P)
            last(Turn(STEPS - 1), LAST_P)

        def node_turns(eng, period):
            for t in (-2, -1, 0, 1):
                period(*(Turn(t + k) if t + k >= 0 else None for k in (2, 1, 0)))
            with eng.Fori(1, (GROUPS - 4) // 2) as half:
                for q in range(2):
                    t = Turn(q, half, 2 + q)
                    period(t.after(2), t.after(1), t)
            for t in range(GROUPS - 4, GROUPS):
                period(*(Turn(t + k) if t + k < GROUPS else None for k in (2, 1, 0)))

        block = ctx.enter_context(nc.Block())

        @block.sync
        def _(sp):
            sp.dma_start(b1_rows[:, :], every_partition(b1)).then_inc(weights_in, 16)
            sp.dma_start(eps_col[:, :], bass.AP(eps_gin.tensor, 0, [[0, P], [1, 1]])).then_inc(weights_in, 16)
            sp.dma_start(g1_rows[:, :], every_partition(g1)).then_inc(weights_in, 16)
            sp.dma_start(bg2_rows[:, :], every_partition(bg2)).then_inc(weights_in, 16)
            sp.dma_start(bf2_rows[:, 0:P], every_partition(bf2)).then_inc(weights_in, 16)
            sp.dma_start(g2_col[:, :], column(g2)).then_inc(weights_in, 16)
            sp.dma_start(b2_col[:, :], column(b2)).then_inc(weights_in, 16)
            sp.dma_start(bg1_col[:, :], column(bg1)).then_inc(weights_in, 16)
            with nc.allow_non_contiguous_dma(reason="one value a partition"):
                sp.dma_start(bf1_col[:, :], bf1.rearrange("(k p) -> p k", p=P)).then_inc(weights_in, 16)
            sp.dma_start(wg1[:, :], Wg1).then_inc(weights_in, 16)
            sp.dma_start(wg2[:, :], Wg2).then_inc(weights_in, 16)
            sp.dma_start(wf1[:, :], Wf1).then_inc(weights_in, 16)
            sp.dma_start(wf2[:, :, :], Wf2.rearrange("(k p) n -> p k n", p=P)).then_inc(weights_in, 16)

            def load_edges(s, parts):
                k = s.slot
                if s.low >= 2:
                    sp.wait_ge(es_dst, s.done(back=2))
                    sp.wait_ge(es_attr, s.done(back=2))
                    sp.wait_ge(gathered[k], s.done_in_slot(16 * TILES, back=2))
                rows = bass.ds(s.row(STEPS * ROWS), parts * TILES)
                sp.dma_start(src_i[k][0:parts, :], src[rows].rearrange("(p j) -> p j", j=TILES)).then_inc(edge_in[k], 16)
                sp.dma_start(dst_i[k][0:parts, :], dst[rows].rearrange("(p j) -> p j", j=TILES)).then_inc(edge_in[k], 16)
                sp.dma_start(dst_row_i[k][0:parts, 0:parts * TILES],
                             dst[rows].rearrange("(o n) -> o n", o=1).to_broadcast([parts, parts * TILES])).then_inc(edge_in[k], 16)
                sp.dma_start(attr[k][0:parts, :, :], rows_of(edge_attr, s, parts)).then_inc(edge_in[k], 16)

            load_edges(Turn(0), P)
            load_edges(Turn(1), P)
            sp.wait_ge(fill_ready, 1)
            part_rows = TABLE // FILL_PARTS
            for part in range(FILL_PARTS):
                there = table[part * part_rows:(part + 1) * part_rows, :].rearrange("(p r) f -> p (r f)", p=P)
                runs = part_rows // P // FILL
                sp.dma_start(there.rearrange("p (r n) -> p r n", r=runs),
                             fill_rows[:, :].rearrange("p (o n) -> p o n", o=1).to_broadcast([P, runs, FILL * P])).then_inc(table_filled, 16)
            edge_turns(sp, lambda s, parts: None,
                       lambda s, parts, parts_next: None if s.low == STEPS - 2 else load_edges(s.after(2), parts if s.low != STEPS - 3 else LAST_P),
                       lambda s, parts: None)

            def store(c):
                k = c.slot
                sp.wait_ge(n_y, c.done())
                if c.low == GROUPS - 1:
                    sp.wait_ge(stored[1 - k], c.after(-1).done_in_slot())
                sp.dma_start(rows_of(out, c), y[k][:, :, :]).then_inc(stored[k], 16)

            def period(a, b, c):
                load(a)
                if c and c.low >= 1:
                    store(c.after(-1))

            def load(a):
                if a is None:
                    return
                nxt = a.after(1)
                if nxt.low < GROUPS:
                    if nxt.low >= 2:
                        sp.wait_ge(n_raw1, nxt.done(back=2))
                        sp.wait_ge(n_u, nxt.done(back=2))
                        sp.wait_ge(n_xb, nxt.done(back=2))
                    sp.dma_start(xn[nxt.slot][:, :, :], rows_of(x, nxt)).then_inc(x_in[nxt.slot], 16)
                if a.low == 0:
                    sp.wait_ge(scattered, 16 * TILES * STEPS)
                if a.low >= 2:
                    sp.wait_ge(n_z, a.done(back=2))
                sp.dma_start(tab[a.slot][:, :, :], rows_of(table, a)).then_inc(tab_in[a.slot], 16)

            sp.dma_start(xn[0][:, :, :], rows_of(x, Turn(0))).then_inc(x_in[0], 16)
            node_turns(sp, period)
            store(Turn(GROUPS - 1))
            sp.wait_ge(stored[0], Turn(GROUPS - 2).done_in_slot())
            sp.wait_ge(stored[1], Turn(GROUPS - 1).done_in_slot())

        @block.gpsimd
        def _(pool):
            nc.gpsimd.memset(ident[:, :], 0.0)
            nc.gpsimd.memset(before[:, :], 1.0)
            nc.gpsimd.memset(ones_col[:, :], 1.0)
            nc.gpsimd.memset(neg_half[:, :], -0.5)
            nc.gpsimd.iota(dummy_row[:, :], [[1, TILES]], base=NODES, channel_multiplier=TILES,
                           allow_small_or_imprecise_dtypes=True).then_inc(consts_set, 1)
            pool.wait_ge(consts_set, 1)
            nc.gpsimd.affine_select(out=ident[:, :], in_=ident[:, :], compare_op=ALU.not_equal, fill=1.0,
                                    base=0, pattern=[[-1, P]], channel_multiplier=1)
            nc.gpsimd.affine_select(out=before[:, :], in_=before[:, :], compare_op=ALU.is_gt, fill=0.0,
                                    base=0, pattern=[[1, P]], channel_multiplier=-1).then_inc(ident_ready, 1)

            def gather(s, parts):
                k = s.slot
                pool.wait_ge(edge_in[k], s.done_in_slot(64))
                if s.low >= 2:
                    pool.wait_ge(es_raw, s.done(back=2))
                    pool.wait_ge(es_u, s.done(back=2))
                nc.gpsimd.nop(nofuse=True)
                for j in range(TILES):
                    nc.gpsimd.indirect_dma_start(xs[k][0:parts, j, :], None, x,
                                                 bass.IndirectOffsetOnAxis(src_i[k][0:parts, j:j + 1], 0)).then_inc(gathered[k], 16)

            def first(s, parts):
                pool.wait_ge(es_arg, s.done())
                nc.gpsimd.tensor_tensor(e_r[0:parts, :], e_arg[0:parts, :], neg_half[0:parts, 0:TILES], ALU.pow).then_inc(es_r, 1)

            def last(s, parts):
                k = s.slot
                pool.wait_ge(es_where, s.done())
                pool.wait_ge(es_out, s.done())
                if s.low == 0:
                    pool.wait_ge(table_filled, 16 * FILL_PARTS)
                else:
                    pool.wait_ge(scattered, s.done(16 * TILES, back=1))
                nc.gpsimd.nop(nofuse=True)
                for j in range(TILES):
                    nc.gpsimd.indirect_dma_start(table, bass.IndirectOffsetOnAxis(where_i[k][0:parts, j:j + 1], 0),
                                                 sums[k][0:parts, j, :], None, compute_op=ALU.add).then_inc(scattered, 16)

            def both(s, parts, parts_next):
                first(s.after(1), parts_next)
                if s.low != STEPS - 2:
                    gather(s.after(2), P if s.low < STEPS - 3 else LAST_P)
                last(s, parts)

            def first_of_all(s, parts):
                gather(s, parts)
                gather(s.after(1), parts)
                first(s, parts)

            edge_turns(pool, first_of_all, both, last)

            def period(a, b, c):
                if a:
                    k = a.slot
                    pool.wait_ge(x_in[k], a.done_in_slot())
                    if a.low == 0:
                        pool.wait_ge(prep, 1)
                    if a.low >= 2:
                        pool.wait_ge(n_res, a.done(back=2))
                    nc.gpsimd.tensor_tensor(xb[k][:, :, :], xn[k][:, :, :], bf2_rows[:, :].rearrange("p (j f) -> p j f", j=TILES),
                                            ALU.add).then_inc(n_xb, 1)
                    pool.wait_ge(n_var2, a.done())
                    if a.low >= 1:
                        pool.wait_ge(n_z, a.done(back=1))
                        pool.wait_ge(n_hb, a.done(back=1))
                    nc.gpsimd.tensor_tensor(r12[:, :], var12[:, :], neg_half[:, :], ALU.pow).then_inc(n_r12, 1)
                if b:
                    k = b.slot
                    pool.wait_ge(n_var3, b.done())
                    if b.low >= 1:
                        pool.wait_ge(n_xn2, b.done(back=1))
                    nc.gpsimd.tensor_tensor(r3[:, :], var3[:, :], neg_half[:, 0:TILES], ALU.pow).then_inc(n_r3, 1)
                    pool.wait_ge(n_r3, b.done())
                    nc.gpsimd.tensor_tensor(nb3[:, :], neg3[:, :], r3[:, :], ALU.mult).then_inc(n_nb3, 1)
                    pool.wait_ge(n_nb3, b.done())
                    if b.low >= 2:
                        pool.wait_ge(n_psx, b.done(back=2))
                    nc.gpsimd.nop(nofuse=True)
                    for j in range(TILES):
                        last_xn2 = nc.gpsimd.tensor_scalar(xn2[k][:, j, :], x2[:, j, :], r3[:, j:j + 1], nb3[:, j:j + 1], ALU.mult, ALU.add)
                    last_xn2.then_inc(n_xn2, 1)
                    pool.wait_ge(n_xb, b.done())
                    if b.low >= 2:
                        pool.wait_ge(n_y, b.done(back=2))
                    nc.gpsimd.tensor_tensor(res[k][:, :, :], xb[k][:, :, :], x2[:, :, :], ALU.add).then_inc(n_res, 1)

            node_turns(pool, period)

        @block.scalar
        def _(act):
            def first(s, parts):
                k = s.slot
                act.wait_ge(es_neg, s.done())
                if s.low >= 1:
                    act.wait_ge(es_w, s.done(back=1))
                for j in range(TILES):
                    last_u = nc.scalar.activation(us[0:parts, j, :], xs[k][0:parts, j, :], ACT.Relu, bias=e_neg[0:parts, j:j + 1])
                last_u.then_inc(es_u, 1)

            def last(s, parts):
                k = s.slot
                act.wait_ge(es_sum, s.done())
                if s.low >= 2:
                    act.wait_ge(scattered, s.done(16 * TILES, back=2))
                nc.scalar.activation(sums[k][0:parts, :, :].rearrange("p j f -> p (j f)"), ps_sum[k][0:parts, :], ACT.Copy).then_inc(es_out, 1)

            def both(s, parts, parts_next):
                first(s.after(1), parts_next)
                last(s, parts)

            edge_turns(act, first, both, last)

            def period(a, b, c):
                if b:
                    act.wait_ge(n_psz, b.done())
                    if b.low >= 1:
                        act.wait_ge(n_psa, b.done(back=1))
                    nc.scalar.activation(zT[:, :], ps_z[:, :], ACT.Copy).then_inc(n_zT, 1)
                if a:
                    act.wait_ge(n_neg1, a.done())
                    if a.low >= 1:
                        act.wait_ge(n_w, a.done(back=1))
                        act.wait_ge(n_hb, a.done(back=1))
                    for j in range(TILES):
                        last_u = nc.scalar.activation(u[:, j, :], xn[a.slot][:, j, :], ACT.Relu, bias=neg1[:, j:j + 1])
                    last_u.then_inc(n_u, 1)
                if b:
                    act.wait_ge(n_psa, b.done())
                    if b.low >= 1:
                        act.wait_ge(n_psg, b.done(back=1))
                    nc.scalar.activation(aT[:, :], ps_a[:, :], ACT.Relu, bias=bg1_col[:, 0:1]).then_inc(n_aT, 1)
                if c:
                    act.wait_ge(n_psx, c.done())
                    if c.low >= 1:
                        act.wait_ge(n_psh, c.done(HC, back=1))
                    nc.scalar.activation(xT_hi[:, :], ps_x[:, :], ACT.Copy).then_inc(n_hi, 1)
                    for h in range(HC):
                        act.wait_ge(n_psh, c.done(HC) - (HC - 1 - h))
                        if c.low >= 1:
                            act.wait_ge(n_used, c.done(HC, back=1) - (HC - 1 - h))
                        nc.scalar.activation(hT[:, h, :], ps_h[h % 3][:, :], ACT.Gelu, bias=bf1_all[:, h:h + 1]).then_inc(n_gelu, 1)

            act.wait_ge(weights_in, 16 * 13)
            act.wait_ge(prep, 2)
            node_turns(act, period)

        @block.vector
        def _(dve):
            dve.wait_ge(weights_in, 16 * 13)
            nc.vector.tensor_scalar(one_eps[:, :], eps_col[:, :], 1.0, None, ALU.add).then_inc(b2_ready, 1)
            dve.wait_ge(b2_ready, 1)
            for r in range(FILL):
                last_fill = nc.vector.tensor_scalar(fill_rows[:, r * P:(r + 1) * P], b1_rows[:, :], one_eps[:, 0:1], None, ALU.mult)
            last_fill.then_inc(fill_ready, 1)
            nc.vector.tensor_scalar(g1_eps[:, :], g1_rows[:, :], one_eps[:, 0:1], None, ALU.mult)
            for j in range(TILES):
                nc.vector.tensor_copy(b1_tiles[:, j * P:(j + 1) * P], b1_rows[:, :])
                if j:
                    last_copy = nc.vector.tensor_copy(bf2_rows[:, j * P:(j + 1) * P], bf2_rows[:, 0:P])
            last_copy.then_inc(prep, 1)
            nc.vector.tensor_scalar(wf1_g[:, :], wf1[:, :], g2_col[:, 0:1], None, ALU.mult).then_inc(b2_ready, 1)
            dve.wait_ge(b2_ready, 2)
            nc.vector.tensor_copy(wf1_hi[:, :], wf1_g[:, :]).then_inc(b2_ready, 1)
            dve.wait_ge(b2_ready, 3)
            nc.vector.tensor_tensor(wf1_lo[:, :], wf1_g[:, :], wf1_hi[:, :].bitcast(f32), ALU.subtract)
            dve.wait_ge(bf1_folded, 1)
            nc.vector.tensor_tensor(bf1_all[:, :], ps_y[:, 0:HC], bf1_col[:, :], ALU.add).then_inc(prep, 1)
            dve.wait_ge(ident_ready, 1)

            def stats(s, parts):
                k = s.slot
                dve.wait_ge(gathered[k], s.done_in_slot(16 * TILES))
                for j in range(TILES):
                    last_raw = nc.vector.bn_stats(e_raw[0:parts, j, :], xs[k][0:parts, j, :])
                last_raw.then_inc(es_raw, 1)
                dve.wait_ge(es_raw, s.done())
                nc.vector.nop(nofuse=True)
                for j in range(TILES):
                    last_mv = nc.vector.bn_aggr(e_mv[0:parts, j, :], e_raw[0:parts, j, :])
                last_mv.then_inc(es_mv, 1)
                dve.wait_ge(es_mv, s.done())
                if s.low >= 1:
                    dve.wait_ge(es_u, s.done(back=1))
                nc.vector.tensor_scalar(e_neg[0:parts, :], e_mv[0:parts, :, 0], -1.0, None, ALU.mult).then_inc(es_neg, 1)
                nc.vector.tensor_scalar(e_var[0:parts, :], e_mv[0:parts, :, 1], LN_EPS, None, ALU.add).then_inc(es_var, 1)
                dve.wait_ge(edge_in[k], s.done_in_slot(64))
                nc.vector.tensor_tensor(attr_b[0:parts, :, :], attr[k][0:parts, :, :],
                                        b1_tiles[0:parts, :].rearrange("p (j f) -> p j f", j=TILES), ALU.add).then_inc(es_attr, 1)

            def second_stats(s, parts):
                dve.wait_ge(es_u, s.done())
                for j in range(TILES):
                    last_raw = nc.vector.bn_stats(e_raw2[0:parts, j, :], us[0:parts, j, :])
                last_raw.then_inc(es_raw2, 1)
                dve.wait_ge(es_raw2, s.done())
                nc.vector.nop(nofuse=True)
                for j in range(TILES):
                    last_mv = nc.vector.bn_aggr(e_mv2[0:parts, j, :], e_raw2[0:parts, j, :])
                last_mv.then_inc(es_mv2, 1)
                dve.wait_ge(es_mv2, s.done())
                dve.wait_ge(es_var, s.done())
                if s.low >= 1:
                    dve.wait_ge(es_r, s.done(back=1))
                nc.vector.scalar_tensor_tensor(out=e_arg[0:parts, :], in0=e_var[0:parts, :], scalar=LN_EPS, in1=e_mv2[0:parts, :, 1],
                                               op0=ALU.mult, op1=ALU.add).then_inc(es_arg, 1)
                for j in range(TILES):
                    last_w = nc.vector.scalar_tensor_tensor(out=ws[0:parts, j, :], in0=us[0:parts, j, :], scalar=e_mv2[0:parts, j, 0:1],
                                                            in1=g1_rows[0:parts, :], op0=ALU.subtract, op1=ALU.mult)
                last_w.then_inc(es_w, 1)

            def message(s, parts):
                k = s.slot
                dve.wait_ge(es_r, s.done())
                dve.wait_ge(es_w, s.done())
                dve.wait_ge(es_attr, s.done())
                for j in range(TILES):
                    last_pre = nc.vector.scalar_tensor_tensor(out=pre[0:parts, j, :], in0=ws[0:parts, j, :], scalar=e_r[0:parts, j:j + 1],
                                                              in1=attr_b[0:parts, j, :], op0=ALU.mult, op1=ALU.add)
                last_pre.then_inc(es_pre, 1)
                dve.wait_ge(es_pre, s.done())
                if s.low >= 2:
                    dve.wait_ge(es_sum, s.done(back=2))
                nc.vector.tensor_scalar(msg[k][0:parts, :, :], pre[0:parts, :, :], 0.0, None, ALU.max).then_inc(es_msg, 1)

            def matches(s, parts):
                k = s.slot
                nc.vector.tensor_copy(dst_f[0:parts, :], dst_i[k][0:parts, :])
                nc.vector.tensor_copy(dst_row[0:parts, :, 0:parts],
                                      dst_row_i[k][0:parts, 0:parts * TILES].rearrange("p (q j) -> p j q", j=TILES)).then_inc(es_dst, 1)
                dve.wait_ge(es_dst, s.done())
                if s.low >= 1:
                    dve.wait_ge(es_sum, s.done(back=1))
                for i in range(TILES):
                    nc.vector.scalar_tensor_tensor(out=same_before[0:parts, i, 0:parts], in0=dst_row[0:parts, i, 0:parts],
                                                   scalar=dst_f[0:parts, i:i + 1], in1=before[0:parts, 0:parts],
                                                   op0=ALU.is_equal, op1=ALU.mult)
                    last_same = nc.vector.tensor_scalar(same[0:parts, i, :].rearrange("p (j q) -> p j q", j=TILES)[:, :, 0:parts],
                                                        dst_row[0:parts, :, 0:parts], dst_f[0:parts, i:i + 1], None, ALU.is_equal)
                last_same.then_inc(es_same, 1)
                nc.vector.tensor_tensor(to_dummy[0:parts, :], dummy_row[0:parts, :], dst_f[0:parts, :], ALU.subtract).then_inc(es_move, 1)

            def rows(s, parts):
                k = s.slot
                dve.wait_ge(es_cnt, s.done())
                dve.wait_ge(es_move, s.done(2) - 1)
                nc.vector.scalar_tensor_tensor(out=move[0:parts, :], in0=ps_cnt[k][0:parts, 0:TILES], scalar=1.0, in1=to_dummy[0:parts, :],
                                               op0=ALU.min, op1=ALU.mult).then_inc(es_move, 1)
                dve.wait_ge(es_move, s.done(2))
                if s.low >= 2:
                    dve.wait_ge(scattered, s.done(16 * TILES, back=2))
                nc.vector.tensor_tensor(where_i[k][0:parts, :], move[0:parts, :], dst_f[0:parts, :], ALU.add).then_inc(es_where, 1)

            def first(s, parts):
                stats(s, parts)
                second_stats(s, parts)
                message(s, parts)

            def both(s, parts, parts_next):
                stats(s.after(1), parts_next)
                matches(s, parts)
                second_stats(s.after(1), parts_next)
                rows(s, parts)
                message(s.after(1), parts_next)

            def last(s, parts):
                matches(s, parts)
                rows(s, parts)

            edge_turns(dve, first, both, last)

            def period(a, b, c):
                if a:
                    k = a.slot
                    dve.wait_ge(x_in[k], a.done_in_slot())
                    for j in range(TILES):
                        last_raw = nc.vector.bn_stats(raw1[:, j, :], xn[k][:, j, :])
                    last_raw.then_inc(n_raw1, 1)
                    dve.wait_ge(n_raw1, a.done())
                    nc.vector.nop(nofuse=True)
                    for j in range(TILES):
                        last_mv = nc.vector.bn_aggr(mv1[:, j, :], raw1[:, j, :])
                    last_mv.then_inc(n_mv1, 1)
                    dve.wait_ge(n_mv1, a.done())
                    if a.low >= 1:
                        dve.wait_ge(n_u, a.done(back=1))
                        dve.wait_ge(n_r12, a.done(back=1))
                    nc.vector.tensor_scalar(neg1[:, :], mv1[:, :, 0], -1.0, None, ALU.mult).then_inc(n_neg1, 1)
                    nc.vector.tensor_scalar(var12[:, 0:TILES], mv1[:, :, 1], LN_EPS, None, ALU.add).then_inc(n_var1, 1)
                if c and (c.low >= 1):
                    finish(c.after(-1))
                if c:
                    dve.wait_ge(n_hi, c.done())
                    if c.low >= 1:
                        dve.wait_ge(n_psh, c.done(HC, back=1))
                    nc.vector.tensor_tensor(xT_lo[:, :], ps_x[:, :], xT_hi[:, :].bitcast(f32), ALU.subtract).then_inc(n_lo, 1)
                if a:
                    dve.wait_ge(n_u, a.done())
                    for j in range(TILES):
                        last_raw = nc.vector.bn_stats(raw2[:, j, :], u[:, j, :])
                    last_raw.then_inc(n_raw2, 1)
                    dve.wait_ge(n_raw2, a.done())
                    nc.vector.nop(nofuse=True)
                    for j in range(TILES):
                        last_mv = nc.vector.bn_aggr(mv2[:, j, :], raw2[:, j, :])
                    last_mv.then_inc(n_mv2, 1)
                    dve.wait_ge(n_mv2, a.done())
                    dve.wait_ge(n_var1, a.done())
                    nc.vector.scalar_tensor_tensor(out=var12[:, TILES:2 * TILES], in0=var12[:, 0:TILES], scalar=LN_EPS, in1=mv2[:, :, 1],
                                                   op0=ALU.mult, op1=ALU.add).then_inc(n_var2, 1)
                if b:
                    k = b.slot
                    dve.wait_ge(n_psg, b.done())
                    dve.wait_ge(n_hb, b.done())
                    if b.low >= 1:
                        dve.wait_ge(n_xn2, b.done(back=1))
                        dve.wait_ge(n_res, b.done(back=1))
                    nc.vector.tensor_tensor(x2[:, :, :], ps_g[:, :].rearrange("p (j f) -> p j f", j=TILES), hb[k][:, :, :], ALU.add).then_inc(n_x2, 1)
                    dve.wait_ge(n_x2, b.done())
                    for j in range(TILES):
                        last_raw = nc.vector.bn_stats(raw3[:, j, :], x2[:, j, :])
                    last_raw.then_inc(n_raw3, 1)
                    dve.wait_ge(n_raw3, b.done())
                    nc.vector.nop(nofuse=True)
                    for j in range(TILES):
                        last_mv = nc.vector.bn_aggr(mv3[:, j, :], raw3[:, j, :])
                    last_mv.then_inc(n_mv3, 1)
                    dve.wait_ge(n_mv3, b.done())
                    nc.vector.tensor_scalar(neg3[:, :], mv3[:, :, 0], -1.0, None, ALU.mult)
                    nc.vector.tensor_scalar(var3[:, :], mv3[:, :, 1], LN_EPS, None, ALU.add).then_inc(n_var3, 1)
                if a:
                    k = a.slot
                    if a.low >= 1:
                        dve.wait_ge(n_z, a.done(back=1))
                    for j in range(TILES):
                        last_w = nc.vector.scalar_tensor_tensor(out=w[:, j, :], in0=u[:, j, :], scalar=mv2[:, j, 0:1], in1=g1_eps[:, :],
                                                                op0=ALU.subtract, op1=ALU.mult)
                    last_w.then_inc(n_w, 1)
                    dve.wait_ge(n_r12, a.done())
                    for j in range(TILES):
                        last_hb = nc.vector.scalar_tensor_tensor(out=hb[k][:, j, :], in0=u[:, j, :], scalar=r12[:, j:j + 1], in1=bg2_rows[:, :],
                                                                 op0=ALU.mult, op1=ALU.add)
                    last_hb.then_inc(n_hb, 1)
                    dve.wait_ge(n_w, a.done())
                    dve.wait_ge(tab_in[k], a.done_in_slot())
                    if a.low >= 2:
                        dve.wait_ge(n_psz, a.done(back=2))
                    for j in range(TILES):
                        last_z = nc.vector.scalar_tensor_tensor(out=z[k][:, j, :], in0=w[:, j, :], scalar=r12[:, TILES + j:TILES + j + 1],
                                                                in1=tab[k][:, j, :], op0=ALU.mult, op1=ALU.add)
                    last_z.then_inc(n_z, 1)

            def finish(c):
                k = c.slot
                dve.wait_ge(n_used, c.done(HC))
                dve.wait_ge(n_res, c.done())
                if c.low >= 2:
                    dve.wait_ge(stored[k], c.done_in_slot(back=2))
                nc.vector.tensor_tensor(y[k][:, :, :], ps_y[:, :].rearrange("p (j f) -> p j f", j=TILES), res[k][:, :, :], ALU.add).then_inc(n_y, 1)

            node_turns(dve, period)
            finish(Turn(GROUPS - 1))

        @block.tensor
        def _(pe):
            pe.wait_ge(weights_in, 16 * 13)
            for h in range(HC):
                last_b = nc.tensor.matmul(ps_y[:, h:h + 1], wf1[:, h * P:(h + 1) * P], b2_col[:, 0:1], start=True, stop=True)
            last_b.then_inc(bf1_folded, 1)

            def last(s, parts):
                k = s.slot
                pe.wait_ge(es_same, s.done())
                if s.low >= 2:
                    pe.wait_ge(es_where, s.done(back=2))
                for j in range(TILES):
                    for i in range(j):
                        nc.tensor.matmul(ps_cnt[k][0:parts, j:j + 1], same[0:parts, i, j * P:j * P + parts], ones_col[0:parts, :],
                                         start=(i == 0), stop=False)
                    last_cnt = nc.tensor.matmul(ps_cnt[k][0:parts, j:j + 1], same_before[0:parts, j, 0:parts], ones_col[0:parts, :],
                                                start=(j == 0), stop=True)
                last_cnt.then_inc(es_cnt, 1)
                pe.wait_ge(es_msg, s.done())
                if s.low >= 2:
                    pe.wait_ge(es_out, s.done(back=2))
                for j in range(TILES):
                    for i in range(TILES):
                        last_sum = nc.tensor.matmul(ps_sum[k][0:parts, j * P:(j + 1) * P], same[0:parts, i, j * P:j * P + parts],
                                                    msg[k][0:parts, i, :], start=(i == 0), stop=(i == TILES - 1))
                last_sum.then_inc(es_sum, 1)

            edge_turns(pe, lambda s, parts: None, lambda s, parts, parts_next: last(s, parts), last)

            def down(c, h):
                pe.wait_ge(n_gelu, c.done(HC) - (HC - 1 - h))
                if h == 0 and c.low >= 1:
                    pe.wait_ge(n_y, c.done(back=1))
                for j in range(TILES):
                    last_y = nc.tensor.matmul(ps_y[:, j * P:(j + 1) * P], hT[:, h, j * P:(j + 1) * P], wf2[:, h, :],
                                              start=(h == 0 and j == 0), stop=(h == HC - 1 and j == TILES - 1), skip_group_check=True)
                last_y.then_inc(n_used, 1)

            def up(c, h):
                if h < 3:
                    if c.low >= 1:
                        pe.wait_ge(n_gelu, c.done(HC, back=1) - (0 if h == 0 else HC - 1 - h))
                else:
                    pe.wait_ge(n_gelu, c.done(HC) - (HC - 1 - (h - 3)))
                for n, (part, lhs) in enumerate(((xT_hi, wf1_hi), (xT_hi, wf1_lo), (xT_lo, wf1_hi))):
                    last_h = nc.tensor.matmul(ps_h[h % 3][:, :], lhs[:, h * P:(h + 1) * P], part[:, :], start=(n == 0), stop=(n == 2))
                last_h.then_inc(n_psh, 1)

            def period(a, b, c):
                if b:
                    pe.wait_ge(n_z, b.done())
                    if b.low >= 1:
                        pe.wait_ge(n_zT, b.done(back=1))
                    for j in range(TILES):
                        last_t = nc.tensor.transpose(ps_z[:, j * P:(j + 1) * P], z[b.slot][:, j, :], ident[:, :])
                    last_t.then_inc(n_psz, 1)
                if c and c.low >= 1:
                    down(c.after(-1), 2)
                if b:
                    pe.wait_ge(n_zT, b.done())
                    if b.low >= 1:
                        pe.wait_ge(n_aT, b.done(back=1))
                    nc.tensor.matmul(ps_a[:, :], wg1[:, :], zT[:, :], start=True, stop=True).then_inc(n_psa, 1)
                if c and c.low >= 1:
                    down(c.after(-1), 3)
                if c:
                    pe.wait_ge(n_xn2, c.done())
                    if c.low >= 1:
                        pe.wait_ge(n_lo, c.done(back=1))
                    for j in range(TILES):
                        last_t = nc.tensor.transpose(ps_x[:, j * P:(j + 1) * P], xn2[c.slot][:, j, :], ident[:, :])
                    last_t.then_inc(n_psx, 1)
                if b:
                    pe.wait_ge(n_aT, b.done())
                    if b.low >= 1:
                        pe.wait_ge(n_x2, b.done(back=1))
                    for j in range(TILES):
                        last_g = nc.tensor.matmul(ps_g[:, j * P:(j + 1) * P], aT[:, j * P:(j + 1) * P], wg2[:, :], start=True, stop=True)
                    last_g.then_inc(n_psg, 1)
                if c:
                    pe.wait_ge(n_lo, c.done())
                    up(c, 0)
                    up(c, 1)
                    up(c, 2)
                    down(c, 0)
                    up(c, 3)
                    down(c, 1)

            node_turns(pe, period)
            down(Turn(GROUPS - 1), 2)
            down(Turn(GROUPS - 1), 3)


_INS = ['x', 'src', 'dst', 'edge_attr_128', 'L0_gnn_g1', 'L0_gnn_b1', 'L0_gnn_g2', 'L0_gnn_b2', 'L0_gnn_eps_gin', 'L0_gnn_Wg1', 'L0_gnn_bg1',
        'L0_gnn_Wg2', 'L0_gnn_bg2', 'L0_gnn_Wf1', 'L0_gnn_bf1', 'L0_gnn_Wf2', 'L0_gnn_bf2']


def kernel(**inputs):
    import numpy as np
    import concourse.bacc as bacc
    from concourse.bass_utils import run_bass_kernel_spmd

    nc = bacc.Bacc("TRN2", target_bir_lowering=False, num_devices=1)
    arrays, args = {}, []
    for name in _INS:
        a = np.ascontiguousarray(inputs[name])
        if a.ndim == 0:
            a = a.reshape(1)
        arrays[f"{name}_dram"] = a
        args.append(nc.dram_tensor(f"{name}_dram", a.shape, mybir.dt.from_np(a.dtype), kind="ExternalInput").ap())
    args.append(nc.dram_tensor("out_dram", inputs['x'].shape, mybir.dt.float32, kind="ExternalOutput").ap())
    gnn_layer(nc, *args)
    return run_bass_kernel_spmd(nc, [arrays], core_ids=[0]).results[0]["out_dram"]
```

```python
import concourse.bass as bass
from concourse import mybir
from contextlib import ExitStack

P = 128
TILES = 4
ROWS = P * TILES


class Turn:

    def __init__(self, q, unroll, lap=0, low=None):
        self.q, self.unroll, self.lap, self.low = q, unroll, lap, q if low is None else low

    def slot(self, ring):
        assert self.unroll % ring == 0
        return self.q % ring

    def done(self, per_turn=1, back=0):
        return self.lap * (self.unroll * per_turn) + (self.q - back + 1) * per_turn

    def done_in_slot(self, ring, per_turn=16, back=0):
        assert back % ring == 0
        return self.lap * (self.unroll // ring * per_turn) + (self.q // ring - back // ring + 1) * per_turn

    def after(self, n):
        return Turn(self.q + n, self.unroll, self.lap, self.low + n)

    def row(self, total):
        if isinstance(self.lap, int):
            return min(self.q * ROWS, total - ROWS)
        return self.lap * (self.unroll * ROWS) + self.q * ROWS


def gnn_layer(nc, x, src, dst, edge_attr, g1, b1, g2, b2, eps_gin, Wg1, bg1, Wg2, bg2, Wf1, bf1, Wf2, bf2, out):
    f32, f32r, i32 = mybir.dt.float32, mybir.dt.float32r, mybir.dt.int32
    ALU, ACT = mybir.AluOpType, mybir.ActivationFunctionType

    NODES, D = x.shape
    EDGES = src.shape[0]
    HIDDEN = Wf1.shape[1]
    HC = HIDDEN // P
    LN_EPS = 1e-5
    GROUPS = -(-NODES // ROWS)
    STEPS = -(-EDGES // ROWS)
    LAST_P = (EDGES - (STEPS - 1) * ROWS) // TILES
    FILL = 8
    FILL_PARTS = 5
    TABLE = -(-(NODES + ROWS) // (P * FILL * FILL_PARTS)) * P * FILL * FILL_PARTS
    assert D == P and HIDDEN % P == 0 and (EDGES - (STEPS - 1) * ROWS) % TILES == 0
    assert NODES >= ROWS and GROUPS % 2 == 0 and GROUPS >= 8 and STEPS % 2 == 1 and STEPS >= 7

    table = nc.dram_tensor("aggregate_table", (TABLE, D), f32).ap()

    ctx = ExitStack()
    with ctx:
        def sb(name, shape, dt=f32):
            return ctx.enter_context(nc.sbuf_tensor(name, shape, dt))

        def pb(name, shape):
            return ctx.enter_context(nc.psum_tensor(name, shape, f32))

        def sem(name):
            return ctx.enter_context(nc.semaphore(name))

        def sem2(name):
            return [sem(f"{name}_{k}") for k in range(2)]

        ident = sb("ident", [P, P])
        before = sb("before", [P, P])
        ones_f = sb("ones_f", [P, 2])
        ones_col = sb("ones_col", [P, 2], f32r)
        neg_half = sb("neg_half", [P, 2 * TILES])
        dummy_row = sb("dummy_row", [P, TILES])
        g1_rows = sb("g1_rows", [P, P])
        b1_rows = sb("b1_rows", [P, P])
        g1_eps = sb("g1_eps", [P, P])
        b1_tiles = sb("b1_tiles", [P, ROWS])
        fill_rows = sb("fill_rows", [P, FILL * P])
        eps_col = sb("eps_col", [P, 1])
        one_eps = sb("one_eps", [P, 1])
        g2_col = sb("g2_col", [P, 1])
        b2_col = sb("b2_col", [P, 1])
        bg1_col = sb("bg1_col", [P, 1])
        bg2_col = sb("bg2_col", [P, 1])
        bf2_col = sb("bf2_col", [P, 1])
        bf1_col = sb("bf1_col", [P, HC])
        bf1_all = sb("bf1_all", [P, HC])
        wg1 = sb("wg1", [P, P])
        wg2 = sb("wg2", [P, P])
        wf1 = sb("wf1", [P, HIDDEN])
        wf1_g = sb("wf1_g", [P, HIDDEN])
        wf1_hi = sb("wf1_hi", [P, HIDDEN], f32r)
        wf1_lo = sb("wf1_lo", [P, HIDDEN], f32r)
        wf2 = sb("wf2", [P, HC, P])

        src_i = [sb(f"src_i{k}", [P, TILES], i32) for k in range(2)]
        dst_i = [sb(f"dst_i{k}", [P, TILES], i32) for k in range(2)]
        dst_row_i = [sb(f"dst_row_i{k}", [P, ROWS], i32) for k in range(2)]
        attr = [sb(f"attr{k}", [P, TILES, P]) for k in range(2)]
        xs = [sb(f"xs{k}", [P, TILES, P]) for k in range(2)]
        us = sb("us", [P, TILES, P])
        ws = sb("ws", [P, TILES, P])
        attr_b = sb("attr_b", [P, TILES, P])
        pre = sb("pre", [P, TILES, P])
        msg = [sb(f"msg{k}", [P, TILES, P]) for k in range(2)]
        e_raw = sb("e_raw", [P, TILES, 6])
        e_raw2 = sb("e_raw2", [P, TILES, 6])
        e_mv = sb("e_mv", [P, TILES, 2])
        e_mv2 = sb("e_mv2", [P, TILES, 2])
        e_neg = sb("e_neg", [P, TILES])
        e_var = sb("e_var", [P, TILES])
        e_arg = sb("e_arg", [P, TILES])
        e_r = sb("e_r", [P, TILES])
        dst_f = sb("dst_f", [P, TILES])
        dst_row = sb("dst_row", [P, TILES, P])
        same = sb("same", [P, TILES, TILES * P], f32r)
        same_before = sb("same_before", [P, TILES, P], f32r)
        to_dummy = sb("to_dummy", [P, TILES])
        move = sb("move", [P, TILES])
        where_i = [sb(f"where_i{k}", [P, TILES], i32) for k in range(2)]
        sums = [sb(f"sums{k}", [P, TILES, P]) for k in range(2)]

        XR = 4
        xn = [sb(f"xn{k}", [P, TILES, P]) for k in range(XR)]
        tab = [sb(f"tab{k}", [P, TILES, P]) for k in range(2)]
        u = [sb(f"u{k}", [P, TILES, P]) for k in range(2)]
        w = sb("w", [P, TILES, P])
        z = [sb(f"z{k}", [P, TILES, P]) for k in range(2)]
        h = [sb(f"h{k}", [P, TILES, P]) for k in range(2)]
        raw1 = sb("raw1", [P, TILES, 6])
        raw2 = sb("raw2", [P, TILES, 6])
        raw3 = sb("raw3", [P, TILES, 6])
        mv1 = sb("mv1", [P, TILES, 2])
        mv2 = sb("mv2", [P, TILES, 2])
        mv3 = sb("mv3", [P, TILES, 2])
        neg1 = [sb(f"neg1_{k}", [P, TILES]) for k in range(2)]
        neg3 = sb("neg3", [P, TILES])
        var12 = [sb(f"var12_{k}", [P, 2 * TILES]) for k in range(2)]
        r12 = [sb(f"r12_{k}", [P, 2 * TILES]) for k in range(2)]
        var3 = sb("var3", [P, TILES])
        r3 = sb("r3", [P, TILES])
        nb3 = sb("nb3", [P, TILES])
        zT = sb("zT", [P, ROWS])
        aT = sb("aT", [P, ROWS])
        gT = sb("gT", [P, ROWS])
        x2 = sb("x2", [P, TILES, P])
        xn2 = [sb(f"xn2_{k}", [P, TILES, P]) for k in range(2)]
        res = [sb(f"res{k}", [P, TILES, P]) for k in range(XR)]
        xT_hi = sb("xT_hi", [P, ROWS], f32r)
        xT_lo = sb("xT_lo", [P, ROWS], f32r)
        hT = sb("hT", [P, HC, ROWS])
        yT = sb("yT", [P, ROWS])
        y = [sb(f"y{k}", [P, TILES, P]) for k in range(2)]

        ps_zy = pb("ps_zy", [P, ROWS])
        ps_x = pb("ps_x", [P, ROWS])
        ps_g = pb("ps_g", [P, ROWS])
        ps_a = pb("ps_a", [P, ROWS])
        ps_h = [pb(f"ps_h{k}", [P, ROWS]) for k in range(3)]
        ps_y = pb("ps_y", [P, ROWS])
        ps_sum = [ps_zy, ps_a]
        ps_cnt = [ps_g, ps_x]

        weights_in, consts_set, ident_ready, prep = sem("weights_in"), sem("consts_set"), sem("ident_ready"), sem("prep")
        b2_ready, bf1_folded, fill_ready, table_filled = sem("b2_ready"), sem("bf1_folded"), sem("fill_ready"), sem("table_filled")
        edge_in, gathered = sem2("edge_in"), sem2("gathered")
        es_raw, es_mv, es_neg, es_u, es_raw2, es_mv2 = (sem(n) for n in ("es_raw", "es_mv", "es_neg", "es_u", "es_raw2", "es_mv2"))
        es_var, es_arg, es_r, es_w, es_attr, es_pre, es_msg = (sem(n) for n in ("es_var", "es_arg", "es_r", "es_w", "es_attr", "es_pre", "es_msg"))
        es_dst, es_same, es_cnt, es_move, es_where, es_sum, es_out = (sem(n) for n in ("es_dst", "es_same", "es_cnt", "es_move", "es_where", "es_sum", "es_out"))
        scattered = sem("scattered")
        x_in, tab_in, stored = [sem(f"x_in_{k}") for k in range(XR)], sem2("tab_in"), sem2("stored")
        n_raw1, n_mv1, n_neg1, n_u, n_raw2, n_mv2 = (sem(n) for n in ("n_raw1", "n_mv1", "n_neg1", "n_u", "n_raw2", "n_mv2"))
        n_var1, n_var2, n_w, n_r12, n_h, n_z = (sem(n) for n in ("n_var1", "n_var2", "n_w", "n_r12", "n_h", "n_z"))
        n_psz, n_zT, n_psa, n_aT, n_psa2, n_gT, n_psg, n_x2 = (sem(n) for n in ("n_psz", "n_zT", "n_psa", "n_aT", "n_psa2", "n_gT", "n_psg", "n_x2"))
        n_raw3, n_mv3, n_var3, n_r3, n_nb3, n_xn2, n_res = (sem(n) for n in ("n_raw3", "n_mv3", "n_var3", "n_r3", "n_nb3", "n_xn2", "n_res"))
        n_psx, n_hi, n_lo, n_psh, n_gelu, n_used, n_yT, n_psy, n_y = (sem(n) for n in ("n_psx", "n_hi", "n_lo", "n_psh", "n_gelu", "n_used", "n_yT", "n_psy", "n_y"))

        def rows_of(tensor, turn, parts=P):
            start = turn.row(NODES if tensor is not edge_attr else STEPS * ROWS)
            return tensor[bass.ds(start, parts * TILES), :].rearrange("(p j) f -> p j f", j=TILES)

        def every_partition(vector, parts=P):
            return bass.AP(vector.tensor, 0, [[0, parts], [1, vector.shape[0]]])

        def column(vector):
            return vector.rearrange("(p o) -> p o", o=1)

        def step(q, lap=0, low=None):
            return Turn(q, 2, lap, low)

        def group(q, lap=0, low=None):
            return Turn(q, 4, lap, low)

        def edge_turns(eng, first, both, last):
            first(step(0), P)
            for s in (0, 1):
                both(step(s), P, P)
            with eng.Fori(1, (STEPS - 3) // 2) as lap:
                for q in range(2):
                    both(step(q, lap, 2 + q), P, P)
            for s in range(STEPS - 3, STEPS - 1):
                both(step(s), P, P if s + 1 < STEPS - 1 else LAST_P)
            last(step(STEPS - 1), LAST_P)

        def node_turns(eng, period):
            first_lap, last_lap = 1, (GROUPS - 6) // 4
            for t in range(-4, 4 * first_lap):
                period(*(group(t + k) if t + k >= 0 else None for k in (4, 3, 2, 1, 0)))
            with eng.Fori(first_lap, last_lap) as lap:
                for q in range(4):
                    period(*(group(q + k, lap, 4 * first_lap + q + k) for k in (4, 3, 2, 1, 0)))
            for t in range(4 * last_lap, GROUPS):
                period(*(group(t + k) if t + k < GROUPS else None for k in (4, 3, 2, 1, 0)))

        block = ctx.enter_context(nc.Block())

        @block.sync
        def _(sp):
            sp.dma_start(b1_rows[:, :], every_partition(b1)).then_inc(weights_in, 16)
            sp.dma_start(eps_col[:, :], bass.AP(eps_gin.tensor, 0, [[0, P], [1, 1]])).then_inc(weights_in, 16)
            sp.dma_start(g1_rows[:, :], every_partition(g1)).then_inc(weights_in, 16)
            sp.dma_start(bg2_col[:, :], column(bg2)).then_inc(weights_in, 16)
            sp.dma_start(bf2_col[:, :], column(bf2)).then_inc(weights_in, 16)
            sp.dma_start(g2_col[:, :], column(g2)).then_inc(weights_in, 16)
            sp.dma_start(b2_col[:, :], column(b2)).then_inc(weights_in, 16)
            sp.dma_start(bg1_col[:, :], column(bg1)).then_inc(weights_in, 16)
            with nc.allow_non_contiguous_dma(reason="one value a partition"):
                sp.dma_start(bf1_col[:, :], bf1.rearrange("(k p) -> p k", p=P)).then_inc(weights_in, 16)
            sp.dma_start(wg1[:, :], Wg1).then_inc(weights_in, 16)
            sp.dma_start(wg2[:, :], Wg2).then_inc(weights_in, 16)
            sp.dma_start(wf1[:, :], Wf1).then_inc(weights_in, 16)
            sp.dma_start(wf2[:, :, :], Wf2.rearrange("(k p) n -> p k n", p=P)).then_inc(weights_in, 16)

            def load_edges(s, parts):
                k = s.slot(2)
                if s.low >= 2:
                    sp.wait_ge(es_dst, s.done(back=2))
                    sp.wait_ge(es_attr, s.done(back=2))
                    sp.wait_ge(gathered[k], s.done_in_slot(2, 16 * TILES, back=2))
                rows = bass.ds(s.row(STEPS * ROWS), parts * TILES)
                sp.dma_start(src_i[k][0:parts, :], src[rows].rearrange("(p j) -> p j", j=TILES)).then_inc(edge_in[k], 16)
                sp.dma_start(dst_i[k][0:parts, :], dst[rows].rearrange("(p j) -> p j", j=TILES)).then_inc(edge_in[k], 16)
                sp.dma_start(dst_row_i[k][0:parts, 0:parts * TILES],
                             dst[rows].rearrange("(o n) -> o n", o=1).to_broadcast([parts, parts * TILES])).then_inc(edge_in[k], 16)
                sp.dma_start(attr[k][0:parts, :, :], rows_of(edge_attr, s, parts)).then_inc(edge_in[k], 16)

            load_edges(step(0), P)
            load_edges(step(1), P)
            sp.wait_ge(fill_ready, 1)
            part_rows = TABLE // FILL_PARTS
            for part in range(FILL_PARTS):
                there = table[part * part_rows:(part + 1) * part_rows, :].rearrange("(p r) f -> p (r f)", p=P)
                runs = part_rows // P // FILL
                sp.dma_start(there.rearrange("p (r n) -> p r n", r=runs),
                             fill_rows[:, :].rearrange("p (o n) -> p o n", o=1).to_broadcast([P, runs, FILL * P])).then_inc(table_filled, 16)
            edge_turns(sp, lambda s, parts: None,
                       lambda s, parts, parts_next: None if s.low == STEPS - 2 else load_edges(s.after(2), parts if s.low != STEPS - 3 else LAST_P),
                       lambda s, parts: None)

            def load_x(g):
                if g.low >= XR:
                    sp.wait_ge(n_res, g.done(back=XR))
                sp.dma_start(xn[g.slot(XR)][:, :, :], rows_of(x, g)).then_inc(x_in[g.slot(XR)], 16)

            def load_tab(g):
                if g.low == 0:
                    sp.wait_ge(scattered, 16 * TILES * STEPS)
                if g.low >= 2:
                    sp.wait_ge(n_z, g.done(back=2))
                sp.dma_start(tab[g.slot(2)][:, :, :], rows_of(table, g)).then_inc(tab_in[g.slot(2)], 16)

            def store(g):
                sp.wait_ge(n_y, g.done())
                if g.low == GROUPS - 1:
                    sp.wait_ge(stored[(GROUPS - 2) % 2], g.after(-1).done_in_slot(2))
                sp.dma_start(rows_of(out, g), y[g.slot(2)][:, :, :]).then_inc(stored[g.slot(2)], 16)

            def period(mean, norm, gin, norm2, mlp):
                if mlp and mlp.low >= 1:
                    store(mlp.after(-1))
                if mean:
                    load_tab(mean)
                    if mean.low + 1 < GROUPS:
                        load_x(mean.after(1))

            load_x(group(0))
            node_turns(sp, period)
            store(group(GROUPS - 1))
            for g in (group(GROUPS - 2), group(GROUPS - 1)):
                sp.wait_ge(stored[g.slot(2)], g.done_in_slot(2))

        @block.gpsimd
        def _(pool):
            nc.gpsimd.memset(ident[:, :], 0.0)
            nc.gpsimd.memset(before[:, :], 1.0)
            nc.gpsimd.memset(ones_f[:, :], 1.0)
            nc.gpsimd.memset(neg_half[:, :], -0.5)
            nc.gpsimd.iota(dummy_row[:, :], [[1, TILES]], base=NODES, channel_multiplier=TILES,
                           allow_small_or_imprecise_dtypes=True).then_inc(consts_set, 1)
            pool.wait_ge(consts_set, 1)
            nc.gpsimd.affine_select(out=ident[:, :], in_=ident[:, :], compare_op=ALU.not_equal, fill=1.0,
                                    base=0, pattern=[[-1, P]], channel_multiplier=1)
            nc.gpsimd.affine_select(out=before[:, :], in_=before[:, :], compare_op=ALU.is_gt, fill=0.0,
                                    base=0, pattern=[[1, P]], channel_multiplier=-1).then_inc(ident_ready, 1)

            def gather(s, parts):
                k = s.slot(2)
                pool.wait_ge(edge_in[k], s.done_in_slot(2, 64))
                if s.low >= 2:
                    pool.wait_ge(es_raw, s.done(back=2))
                    pool.wait_ge(es_u, s.done(back=2))
                nc.gpsimd.nop(nofuse=True)
                for j in range(TILES):
                    nc.gpsimd.indirect_dma_start(xs[k][0:parts, j, :], None, x,
                                                 bass.IndirectOffsetOnAxis(src_i[k][0:parts, j:j + 1], 0)).then_inc(gathered[k], 16)

            def first(s, parts):
                pool.wait_ge(es_arg, s.done())
                nc.gpsimd.tensor_tensor(e_r[0:parts, :], e_arg[0:parts, :], neg_half[0:parts, 0:TILES], ALU.pow).then_inc(es_r, 1)

            def last(s, parts):
                k = s.slot(2)
                pool.wait_ge(es_where, s.done())
                pool.wait_ge(es_out, s.done())
                if s.low == 0:
                    pool.wait_ge(table_filled, 16 * FILL_PARTS)
                else:
                    pool.wait_ge(scattered, s.done(16 * TILES, back=1))
                nc.gpsimd.nop(nofuse=True)
                for j in range(TILES):
                    nc.gpsimd.indirect_dma_start(table, bass.IndirectOffsetOnAxis(where_i[k][0:parts, j:j + 1], 0),
                                                 sums[k][0:parts, j, :], None, compute_op=ALU.add).then_inc(scattered, 16)

            def both(s, parts, parts_next):
                first(s.after(1), parts_next)
                if s.low != STEPS - 2:
                    gather(s.after(2), P if s.low < STEPS - 3 else LAST_P)
                last(s, parts)

            def first_of_all(s, parts):
                gather(s, parts)
                gather(s.after(1), parts)
                first(s, parts)

            edge_turns(pool, first_of_all, both, last)

            def period(mean, norm, gin, norm2, mlp):
                if norm2:
                    g = norm2
                    pool.wait_ge(n_var3, g.done())
                    if g.low >= 1:
                        pool.wait_ge(n_xn2, g.done(back=1))
                    nc.gpsimd.tensor_tensor(r3[:, :], var3[:, :], neg_half[:, 0:TILES], ALU.pow).then_inc(n_r3, 1)
                    pool.wait_ge(n_r3, g.done())
                    nc.gpsimd.tensor_tensor(nb3[:, :], neg3[:, :], r3[:, :], ALU.mult).then_inc(n_nb3, 1)
                    pool.wait_ge(n_nb3, g.done())
                    if g.low >= 2:
                        pool.wait_ge(n_psx, g.done(back=2))
                    nc.gpsimd.nop(nofuse=True)
                    for j in range(TILES):
                        last_xn2 = nc.gpsimd.tensor_scalar(xn2[g.slot(2)][:, j, :], x2[:, j, :], r3[:, j:j + 1], nb3[:, j:j + 1], ALU.mult, ALU.add)
                    last_xn2.then_inc(n_xn2, 1)
                if norm:
                    g = norm
                    pool.wait_ge(n_var2, g.done())
                    k = g.slot(2)
                    if g.low >= 2:
                        pool.wait_ge(n_z, g.done(back=2))
                        pool.wait_ge(n_h, g.done(back=2))
                    nc.gpsimd.tensor_tensor(r12[k][:, :], var12[k][:, :], neg_half[:, :], ALU.pow).then_inc(n_r12, 1)
                if norm2:
                    g = norm2
                    pool.wait_ge(n_x2, g.done())
                    if g.low >= XR:
                        pool.wait_ge(n_y, g.done(back=XR))
                    nc.gpsimd.tensor_tensor(res[g.slot(XR)][:, :, :], xn[g.slot(XR)][:, :, :], x2[:, :, :], ALU.add).then_inc(n_res, 1)

            node_turns(pool, period)

        @block.scalar
        def _(act):
            def first(s, parts):
                k = s.slot(2)
                act.wait_ge(es_neg, s.done())
                if s.low >= 1:
                    act.wait_ge(es_w, s.done(back=1))
                for j in range(TILES):
                    last_u = nc.scalar.activation(us[0:parts, j, :], xs[k][0:parts, j, :], ACT.Relu, bias=e_neg[0:parts, j:j + 1])
                last_u.then_inc(es_u, 1)

            def last(s, parts):
                k = s.slot(2)
                act.wait_ge(es_sum, s.done())
                if s.low >= 2:
                    act.wait_ge(scattered, s.done(16 * TILES, back=2))
                nc.scalar.activation(sums[k][0:parts, :, :].rearrange("p j f -> p (j f)"), ps_sum[k][0:parts, :], ACT.Copy).then_inc(es_out, 1)

            def both(s, parts, parts_next):
                first(s.after(1), parts_next)
                last(s, parts)

            edge_turns(act, first, both, last)

            def mlp_out(g):
                act.wait_ge(n_used, g.done(HC))
                if g.low >= 1:
                    act.wait_ge(n_psy, g.done(back=1))
                nc.scalar.activation(yT[:, :], ps_y[:, :], ACT.Identity, bias=bf2_col[:, 0:1]).then_inc(n_yT, 1)

            def gelu(g, c):
                act.wait_ge(n_psh, g.done(HC) - (HC - 1 - c))
                if g.low >= 1:
                    act.wait_ge(n_used, g.done(HC, back=1) - (HC - 1 - c))
                nc.scalar.activation(hT[:, c, :], ps_h[c % 3][:, :], ACT.Gelu, bias=bf1_all[:, c:c + 1]).then_inc(n_gelu, 1)

            def period(mean, norm, gin, norm2, mlp):
                if mlp and mlp.low >= 1:
                    mlp_out(mlp.after(-1))
                if gin:
                    act.wait_ge(n_psz, gin.done())
                    if gin.low >= 1:
                        act.wait_ge(n_psa, gin.done(back=1))
                    nc.scalar.activation(zT[:, :], ps_zy[:, :], ACT.Copy).then_inc(n_zT, 1)
                if mlp:
                    gelu(mlp, 0)
                if gin:
                    g = gin
                    act.wait_ge(n_psa, g.done())
                    if g.low >= 1:
                        act.wait_ge(n_psa2, g.done(back=1))
                    nc.scalar.activation(aT[:, :], ps_a[:, :], ACT.Relu, bias=bg1_col[:, 0:1]).then_inc(n_aT, 1)
                    act.wait_ge(n_r12, g.done())
                    if g.low >= 2:
                        act.wait_ge(n_x2, g.done(back=2))
                    for j in range(TILES):
                        last_h = nc.scalar.activation(h[g.slot(2)][:, j, :], u[g.slot(2)][:, j, :], ACT.Relu, scale=r12[g.slot(2)][:, j:j + 1])
                    last_h.then_inc(n_h, 1)
                if mlp:
                    gelu(mlp, 1)
                    gelu(mlp, 2)
                if gin:
                    act.wait_ge(n_psa2, gin.done())
                    if gin.low >= 1:
                        act.wait_ge(n_psg, gin.done(back=1))
                    nc.scalar.activation(gT[:, :], ps_a[:, :], ACT.Identity, bias=bg2_col[:, 0:1]).then_inc(n_gT, 1)
                if mlp:
                    gelu(mlp, 3)
                if mean:
                    g = mean
                    act.wait_ge(n_neg1, g.done())
                    if g.low >= 2:
                        act.wait_ge(n_w, g.done(back=2))
                        act.wait_ge(n_h, g.done(back=2))
                    for j in range(TILES):
                        last_u = nc.scalar.activation(u[g.slot(2)][:, j, :], xn[g.slot(XR)][:, j, :], ACT.Relu, bias=neg1[g.slot(2)][:, j:j + 1])
                    last_u.then_inc(n_u, 1)
                if norm2:
                    g = norm2
                    act.wait_ge(n_psx, g.done())
                    if g.low >= 1:
                        act.wait_ge(n_psh, g.done(HC, back=1))
                    nc.scalar.activation(xT_hi[:, :], ps_x[:, :], ACT.Copy).then_inc(n_hi, 1)

            act.wait_ge(weights_in, 16 * 13)
            act.wait_ge(prep, 1)
            node_turns(act, period)
            mlp_out(group(GROUPS - 1))

        @block.vector
        def _(dve):
            dve.wait_ge(weights_in, 16 * 13)
            nc.vector.tensor_scalar(one_eps[:, :], eps_col[:, :], 1.0, None, ALU.add).then_inc(b2_ready, 1)
            dve.wait_ge(b2_ready, 1)
            for r in range(FILL):
                last_fill = nc.vector.tensor_scalar(fill_rows[:, r * P:(r + 1) * P], b1_rows[:, :], one_eps[:, 0:1], None, ALU.mult)
            last_fill.then_inc(fill_ready, 1)
            nc.vector.tensor_scalar(g1_eps[:, :], g1_rows[:, :], one_eps[:, 0:1], None, ALU.mult)
            for j in range(TILES):
                nc.vector.tensor_copy(b1_tiles[:, j * P:(j + 1) * P], b1_rows[:, :])
            nc.vector.tensor_scalar(wf1_g[:, :], wf1[:, :], g2_col[:, 0:1], None, ALU.mult).then_inc(b2_ready, 1)
            dve.wait_ge(b2_ready, 2)
            nc.vector.tensor_copy(wf1_hi[:, :], wf1_g[:, :]).then_inc(b2_ready, 1)
            dve.wait_ge(b2_ready, 3)
            nc.vector.tensor_tensor(wf1_lo[:, :], wf1_g[:, :], wf1_hi[:, :].bitcast(f32), ALU.subtract)
            dve.wait_ge(bf1_folded, 1)
            nc.vector.tensor_tensor(bf1_all[:, :], ps_y[:, 0:HC], bf1_col[:, :], ALU.add).then_inc(prep, 1)
            dve.wait_ge(ident_ready, 1)
            nc.vector.tensor_copy(ones_col[:, :], ones_f[:, :])

            def stats(s, parts):
                k = s.slot(2)
                dve.wait_ge(gathered[k], s.done_in_slot(2, 16 * TILES))
                for j in range(TILES):
                    last_raw = nc.vector.bn_stats(e_raw[0:parts, j, :], xs[k][0:parts, j, :])
                last_raw.then_inc(es_raw, 1)
                dve.wait_ge(es_raw, s.done())
                nc.vector.nop(nofuse=True)
                for j in range(TILES):
                    last_mv = nc.vector.bn_aggr(e_mv[0:parts, j, :], e_raw[0:parts, j, :])
                last_mv.then_inc(es_mv, 1)
                dve.wait_ge(es_mv, s.done())
                if s.low >= 1:
                    dve.wait_ge(es_u, s.done(back=1))
                nc.vector.tensor_scalar(e_neg[0:parts, :], e_mv[0:parts, :, 0], -1.0, None, ALU.mult).then_inc(es_neg, 1)
                nc.vector.tensor_scalar(e_var[0:parts, :], e_mv[0:parts, :, 1], LN_EPS, None, ALU.add).then_inc(es_var, 1)
                dve.wait_ge(edge_in[k], s.done_in_slot(2, 64))
                nc.vector.tensor_tensor(attr_b[0:parts, :, :], attr[k][0:parts, :, :],
                                        b1_tiles[0:parts, :].rearrange("p (j f) -> p j f", j=TILES), ALU.add).then_inc(es_attr, 1)

            def second_stats(s, parts):
                dve.wait_ge(es_u, s.done())
                for j in range(TILES):
                    last_raw = nc.vector.bn_stats(e_raw2[0:parts, j, :], us[0:parts, j, :])
                last_raw.then_inc(es_raw2, 1)
                dve.wait_ge(es_raw2, s.done())
                nc.vector.nop(nofuse=True)
                for j in range(TILES):
                    last_mv = nc.vector.bn_aggr(e_mv2[0:parts, j, :], e_raw2[0:parts, j, :])
                last_mv.then_inc(es_mv2, 1)
                dve.wait_ge(es_mv2, s.done())
                dve.wait_ge(es_var, s.done())
                if s.low >= 1:
                    dve.wait_ge(es_r, s.done(back=1))
                nc.vector.scalar_tensor_tensor(out=e_arg[0:parts, :], in0=e_var[0:parts, :], scalar=LN_EPS, in1=e_mv2[0:parts, :, 1],
                                               op0=ALU.mult, op1=ALU.add).then_inc(es_arg, 1)
                for j in range(TILES):
                    last_w = nc.vector.scalar_tensor_tensor(out=ws[0:parts, j, :], in0=us[0:parts, j, :], scalar=e_mv2[0:parts, j, 0:1],
                                                            in1=g1_rows[0:parts, :], op0=ALU.subtract, op1=ALU.mult)
                last_w.then_inc(es_w, 1)

            def message(s, parts):
                k = s.slot(2)
                dve.wait_ge(es_r, s.done())
                dve.wait_ge(es_w, s.done())
                dve.wait_ge(es_attr, s.done())
                for j in range(TILES):
                    last_pre = nc.vector.scalar_tensor_tensor(out=pre[0:parts, j, :], in0=ws[0:parts, j, :], scalar=e_r[0:parts, j:j + 1],
                                                              in1=attr_b[0:parts, j, :], op0=ALU.mult, op1=ALU.add)
                last_pre.then_inc(es_pre, 1)
                dve.wait_ge(es_pre, s.done())
                if s.low >= 2:
                    dve.wait_ge(es_sum, s.done(back=2))
                nc.vector.tensor_scalar(msg[k][0:parts, :, :], pre[0:parts, :, :], 0.0, None, ALU.max).then_inc(es_msg, 1)

            def matches(s, parts):
                k = s.slot(2)
                nc.vector.tensor_copy(dst_f[0:parts, :], dst_i[k][0:parts, :])
                nc.vector.tensor_copy(dst_row[0:parts, :, 0:parts],
                                      dst_row_i[k][0:parts, 0:parts * TILES].rearrange("p (q j) -> p j q", j=TILES)).then_inc(es_dst, 1)
                dve.wait_ge(es_dst, s.done())
                if s.low >= 1:
                    dve.wait_ge(es_sum, s.done(back=1))
                for i in range(TILES):
                    nc.vector.scalar_tensor_tensor(out=same_before[0:parts, i, 0:parts], in0=dst_row[0:parts, i, 0:parts],
                                                   scalar=dst_f[0:parts, i:i + 1], in1=before[0:parts, 0:parts],
                                                   op0=ALU.is_equal, op1=ALU.mult)
                    last_same = nc.vector.tensor_scalar(same[0:parts, i, :].rearrange("p (j q) -> p j q", j=TILES)[:, :, 0:parts],
                                                        dst_row[0:parts, :, 0:parts], dst_f[0:parts, i:i + 1], None, ALU.is_equal)
                last_same.then_inc(es_same, 1)
                nc.vector.tensor_tensor(to_dummy[0:parts, :], dummy_row[0:parts, :], dst_f[0:parts, :], ALU.subtract).then_inc(es_move, 1)

            def rows(s, parts):
                k = s.slot(2)
                dve.wait_ge(es_cnt, s.done())
                dve.wait_ge(es_move, s.done(2) - 1)
                nc.vector.scalar_tensor_tensor(out=move[0:parts, :], in0=ps_cnt[k][0:parts, 0:2 * TILES:2], scalar=1.0, in1=to_dummy[0:parts, :],
                                               op0=ALU.min, op1=ALU.mult).then_inc(es_move, 1)
                dve.wait_ge(es_move, s.done(2))
                if s.low >= 2:
                    dve.wait_ge(scattered, s.done(16 * TILES, back=2))
                nc.vector.tensor_tensor(where_i[k][0:parts, :], move[0:parts, :], dst_f[0:parts, :], ALU.add).then_inc(es_where, 1)

            def first(s, parts):
                stats(s, parts)
                second_stats(s, parts)
                message(s, parts)

            def both(s, parts, parts_next):
                stats(s.after(1), parts_next)
                matches(s, parts)
                second_stats(s.after(1), parts_next)
                rows(s, parts)
                message(s.after(1), parts_next)

            def last(s, parts):
                matches(s, parts)
                rows(s, parts)

            edge_turns(dve, first, both, last)

            def finish(g):
                k = g.slot(2)
                dve.wait_ge(n_psy, g.done())
                dve.wait_ge(n_res, g.done())
                if g.low >= 2:
                    dve.wait_ge(stored[k], g.done_in_slot(2, back=2))
                nc.vector.tensor_tensor(y[k][:, :, :], ps_zy[:, :].rearrange("p (j f) -> p j f", j=TILES), res[g.slot(XR)][:, :, :], ALU.add).then_inc(n_y, 1)

            def period(mean, norm, gin, norm2, mlp):
                if norm2:
                    g = norm2
                    dve.wait_ge(n_psg, g.done())
                    dve.wait_ge(n_h, g.done())
                    if g.low >= 1:
                        dve.wait_ge(n_xn2, g.done(back=1))
                        dve.wait_ge(n_res, g.done(back=1))
                    nc.vector.tensor_tensor(x2[:, :, :], ps_g[:, :].rearrange("p (j f) -> p j f", j=TILES), h[g.slot(2)][:, :, :], ALU.add).then_inc(n_x2, 1)
                if norm:
                    dve.wait_ge(n_u, norm.done())
                    for j in range(TILES):
                        last_raw = nc.vector.bn_stats(raw2[:, j, :], u[norm.slot(2)][:, j, :])
                    last_raw.then_inc(n_raw2, 1)
                if norm2:
                    dve.wait_ge(n_x2, norm2.done())
                    for j in range(TILES):
                        last_raw = nc.vector.bn_stats(raw3[:, j, :], x2[:, j, :])
                    last_raw.then_inc(n_raw3, 1)
                if norm:
                    dve.wait_ge(n_raw2, norm.done())
                    nc.vector.nop(nofuse=True)
                    for j in range(TILES):
                        last_mv = nc.vector.bn_aggr(mv2[:, j, :], raw2[:, j, :])
                    last_mv.then_inc(n_mv2, 1)
                if norm2:
                    dve.wait_ge(n_raw3, norm2.done())
                    nc.vector.nop(nofuse=True)
                    for j in range(TILES):
                        last_mv = nc.vector.bn_aggr(mv3[:, j, :], raw3[:, j, :])
                    last_mv.then_inc(n_mv3, 1)
                if norm:
                    dve.wait_ge(n_mv2, norm.done())
                    dve.wait_ge(n_var1, norm.done())
                    nc.vector.scalar_tensor_tensor(out=var12[norm.slot(2)][:, TILES:2 * TILES], in0=var12[norm.slot(2)][:, 0:TILES], scalar=LN_EPS, in1=mv2[:, :, 1],
                                                   op0=ALU.mult, op1=ALU.add).then_inc(n_var2, 1)
                if norm2:
                    dve.wait_ge(n_mv3, norm2.done())
                    nc.vector.tensor_scalar(neg3[:, :], mv3[:, :, 0], -1.0, None, ALU.mult)
                    nc.vector.tensor_scalar(var3[:, :], mv3[:, :, 1], LN_EPS, None, ALU.add).then_inc(n_var3, 1)
                if mean:
                    g = mean
                    dve.wait_ge(x_in[g.slot(XR)], g.done_in_slot(XR))
                    for j in range(TILES):
                        last_raw = nc.vector.bn_stats(raw1[:, j, :], xn[g.slot(XR)][:, j, :])
                    last_raw.then_inc(n_raw1, 1)
                if mlp and mlp.low >= 1:
                    finish(mlp.after(-1))
                if mean:
                    dve.wait_ge(n_raw1, mean.done())
                    nc.vector.nop(nofuse=True)
                    for j in range(TILES):
                        last_mv = nc.vector.bn_aggr(mv1[:, j, :], raw1[:, j, :])
                    last_mv.then_inc(n_mv1, 1)
                if norm:
                    if norm.low >= 1:
                        dve.wait_ge(n_z, norm.done(back=1))
                    for j in range(TILES):
                        last_w = nc.vector.scalar_tensor_tensor(out=w[:, j, :], in0=u[norm.slot(2)][:, j, :], scalar=mv2[:, j, 0:1], in1=g1_eps[:, :],
                                                                op0=ALU.subtract, op1=ALU.mult)
                    last_w.then_inc(n_w, 1)
                if mean:
                    dve.wait_ge(n_mv1, mean.done())
                    k = mean.slot(2)
                    if mean.low >= 2:
                        dve.wait_ge(n_u, mean.done(back=2))
                        dve.wait_ge(n_r12, mean.done(back=2))
                    nc.vector.tensor_scalar(neg1[k][:, :], mv1[:, :, 0], -1.0, None, ALU.mult).then_inc(n_neg1, 1)
                    nc.vector.tensor_scalar(var12[k][:, 0:TILES], mv1[:, :, 1], LN_EPS, None, ALU.add).then_inc(n_var1, 1)
                if norm:
                    g, k = norm, norm.slot(2)
                    dve.wait_ge(n_r12, g.done())
                    dve.wait_ge(n_w, g.done())
                    dve.wait_ge(tab_in[k], g.done_in_slot(2))
                    if g.low >= 2:
                        dve.wait_ge(n_psz, g.done(back=2))
                    for j in range(TILES):
                        last_z = nc.vector.scalar_tensor_tensor(out=z[k][:, j, :], in0=w[:, j, :], scalar=r12[k][:, TILES + j:TILES + j + 1],
                                                                in1=tab[k][:, j, :], op0=ALU.mult, op1=ALU.add)
                    last_z.then_inc(n_z, 1)
                if norm2:
                    g = norm2
                    dve.wait_ge(n_hi, g.done())
                    if g.low >= 1:
                        dve.wait_ge(n_psh, g.done(HC, back=1))
                    nc.vector.tensor_tensor(xT_lo[:, :], ps_x[:, :], xT_hi[:, :].bitcast(f32), ALU.subtract).then_inc(n_lo, 1)

            node_turns(dve, period)
            finish(group(GROUPS - 1))

        @block.tensor
        def _(pe):
            pe.wait_ge(weights_in, 16 * 13)
            for h in range(HC):
                last_b = nc.tensor.matmul(ps_y[:, h:h + 1], wf1[:, h * P:(h + 1) * P], b2_col[:, 0:1], start=True, stop=True)
            last_b.then_inc(bf1_folded, 1)

            def last(s, parts):
                k = s.slot(2)
                pe.wait_ge(es_same, s.done())
                if s.low >= 2:
                    pe.wait_ge(es_where, s.done(back=2))
                for j in range(TILES):
                    for i in range(j):
                        nc.tensor.matmul(ps_cnt[k][:, 2 * j:2 * j + 2], same[0:parts, i, j * P:(j + 1) * P], ones_col[0:parts, :],
                                         start=(i == 0), stop=False)
                    last_cnt = nc.tensor.matmul(ps_cnt[k][:, 2 * j:2 * j + 2], same_before[0:parts, j, :], ones_col[0:parts, :],
                                                start=(j == 0), stop=True)
                last_cnt.then_inc(es_cnt, 1)
                pe.wait_ge(es_msg, s.done())
                if s.low >= 2:
                    pe.wait_ge(es_out, s.done(back=2))
                for j in range(TILES):
                    for i in range(TILES):
                        last_sum = nc.tensor.matmul(ps_sum[k][0:parts, j * P:(j + 1) * P], same[0:parts, i, j * P:j * P + parts].bitcast(f32),
                                                    msg[k][0:parts, i, :], start=(i == 0), stop=(i == TILES - 1))
                last_sum.then_inc(es_sum, 1)

            edge_turns(pe, lambda s, parts: None, lambda s, parts, parts_next: last(s, parts), last)

            def transposes(bank, rows):
                for j in range(TILES):
                    last_t = nc.tensor.transpose(bank[:, j * P:(j + 1) * P], rows[:, j * P:(j + 1) * P], ident[:, :])
                return last_t

            def flat(tiles):
                return tiles[:, :, :].rearrange("p j f -> p (j f)")

            def up(g, c):
                if c < 3:
                    if g.low >= 1:
                        pe.wait_ge(n_gelu, g.done(HC, back=1) - (0 if c == 0 else HC - 1 - c))
                else:
                    pe.wait_ge(n_gelu, g.done(HC) - (HC - 1 - (c - 3)))
                for n, (part, lhs) in enumerate(((xT_hi, wf1_hi), (xT_hi, wf1_lo), (xT_lo, wf1_hi))):
                    last_h = nc.tensor.matmul(ps_h[c % 3][:, :], lhs[:, c * P:(c + 1) * P], part[:, :], start=(n == 0), stop=(n == 2))
                last_h.then_inc(n_psh, 1)

            def down(g, c):
                pe.wait_ge(n_gelu, g.done(HC) - (HC - 1 - c))
                if c == 0 and g.low >= 1:
                    pe.wait_ge(n_yT, g.done(back=1))
                nc.tensor.matmul(ps_y[:, :], wf2[:, c, :], hT[:, c, :], start=(c == 0), stop=(c == HC - 1)).then_inc(n_used, 1)

            def mlp_rows(g):
                pe.wait_ge(n_yT, g.done())
                if g.low + 3 < GROUPS:
                    pe.wait_ge(n_zT, g.after(3).done())
                else:
                    pe.wait_ge(n_y, g.done(back=1))
                transposes(ps_zy, yT).then_inc(n_psy, 1)

            def period(mean, norm, gin, norm2, mlp):
                if gin:
                    g = gin
                    pe.wait_ge(n_z, g.done())
                    if g.low >= 4:
                        pe.wait_ge(n_y, g.done(back=4))
                    elif g.low >= 1:
                        pe.wait_ge(n_zT, g.done(back=1))
                    transposes(ps_zy, flat(z[g.slot(2)])).then_inc(n_psz, 1)
                if mlp:
                    pe.wait_ge(n_lo, mlp.done())
                    up(mlp, 0)
                    if mlp.low >= 1:
                        mlp_rows(mlp.after(-1))
                if gin:
                    g = gin
                    pe.wait_ge(n_zT, g.done())
                    if g.low >= 1:
                        pe.wait_ge(n_gT, g.done(back=1))
                    nc.tensor.matmul(ps_a[:, :], wg1[:, :], zT[:, :], start=True, stop=True).then_inc(n_psa, 1)
                if mlp:
                    up(mlp, 1)
                    up(mlp, 2)
                if gin:
                    pe.wait_ge(n_aT, gin.done())
                    nc.tensor.matmul(ps_a[:, :], wg2[:, :], aT[:, :], start=True, stop=True).then_inc(n_psa2, 1)
                if mlp:
                    down(mlp, 0)
                    up(mlp, 3)
                    down(mlp, 1)
                if gin:
                    g = gin
                    pe.wait_ge(n_gT, g.done())
                    if g.low >= 1:
                        pe.wait_ge(n_x2, g.done(back=1))
                    transposes(ps_g, gT).then_inc(n_psg, 1)
                if mlp:
                    down(mlp, 2)
                if norm2:
                    g = norm2
                    pe.wait_ge(n_xn2, g.done())
                    if g.low >= 1:
                        pe.wait_ge(n_lo, g.done(back=1))
                    transposes(ps_x, flat(xn2[g.slot(2)])).then_inc(n_psx, 1)
                if mlp:
                    down(mlp, 3)

            node_turns(pe, period)
            mlp_rows(group(GROUPS - 1))


_INS = ['x', 'src', 'dst', 'edge_attr_128', 'L0_gnn_g1', 'L0_gnn_b1', 'L0_gnn_g2', 'L0_gnn_b2', 'L0_gnn_eps_gin', 'L0_gnn_Wg1', 'L0_gnn_bg1',
        'L0_gnn_Wg2', 'L0_gnn_bg2', 'L0_gnn_Wf1', 'L0_gnn_bf1', 'L0_gnn_Wf2', 'L0_gnn_bf2']


def kernel(**inputs):
    import numpy as np
    import concourse.bacc as bacc
    from concourse.bass_utils import run_bass_kernel_spmd

    nc = bacc.Bacc("TRN2", target_bir_lowering=False, num_devices=1)
    arrays, args = {}, []
    for name in _INS:
        a = np.ascontiguousarray(inputs[name])
        if a.ndim == 0:
            a = a.reshape(1)
        arrays[f"{name}_dram"] = a
        args.append(nc.dram_tensor(f"{name}_dram", a.shape, mybir.dt.from_np(a.dtype), kind="ExternalInput").ap())
    args.append(nc.dram_tensor("out_dram", inputs['x'].shape, mybir.dt.float32, kind="ExternalOutput").ap())
    gnn_layer(nc, *args)
    return run_bass_kernel_spmd(nc, [arrays], core_ids=[0]).results[0]["out_dram"]
```

```python
import concourse.bass as bass
from concourse import mybir
from contextlib import ExitStack

P = 128
TILES = 4
ROWS = P * TILES


class Turn:

    def __init__(self, q, unroll, lap=0, low=None):
        self.q, self.unroll, self.lap, self.low = q, unroll, lap, q if low is None else low

    def slot(self, ring):
        assert self.unroll % ring == 0
        return self.q % ring

    def done(self, per_turn=1, back=0):
        return self.lap * (self.unroll * per_turn) + (self.q - back + 1) * per_turn

    def done_in_slot(self, ring, per_turn=16, back=0):
        assert back % ring == 0
        return self.lap * (self.unroll // ring * per_turn) + (self.q // ring - back // ring + 1) * per_turn

    def after(self, n):
        return Turn(self.q + n, self.unroll, self.lap, self.low + n)

    def row(self, total):
        if isinstance(self.lap, int):
            return min(self.q * ROWS, total - ROWS)
        return self.lap * (self.unroll * ROWS) + self.q * ROWS


def gnn_layer(nc, x, src, dst, edge_attr, g1, b1, g2, b2, eps_gin, Wg1, bg1, Wg2, bg2, Wf1, bf1, Wf2, bf2, out):
    f32, f32r, i32 = mybir.dt.float32, mybir.dt.float32r, mybir.dt.int32
    ALU, ACT = mybir.AluOpType, mybir.ActivationFunctionType

    NODES, D = x.shape
    EDGES = src.shape[0]
    HIDDEN = Wf1.shape[1]
    HC = HIDDEN // P
    SPLIT = 2
    DOWN_ORDER = (*range(SPLIT, HC), *range(SPLIT))
    LN_EPS = 1e-5
    GROUPS = -(-NODES // ROWS)
    STEPS = -(-EDGES // ROWS)
    LAST_P = (EDGES - (STEPS - 1) * ROWS) // TILES
    FILL = 8
    FILL_PARTS = 25
    TABLE = -(-(NODES + ROWS) // (P * FILL * FILL_PARTS)) * P * FILL * FILL_PARTS
    assert D == P and HIDDEN % P == 0 and (EDGES - (STEPS - 1) * ROWS) % TILES == 0
    assert NODES >= ROWS and GROUPS % 2 == 0 and GROUPS >= 8 and STEPS >= 20

    table = nc.dram_tensor("aggregate_table", (TABLE, D), f32).ap()

    ctx = ExitStack()
    with ctx:
        def sb(name, shape, dt=f32):
            return ctx.enter_context(nc.sbuf_tensor(name, shape, dt))

        def pb(name, shape):
            return ctx.enter_context(nc.psum_tensor(name, shape, f32))

        def sem(name):
            return ctx.enter_context(nc.semaphore(name))

        def sem2(name):
            return [sem(f"{name}_{k}") for k in range(2)]

        ident = sb("ident", [P, P])
        before = sb("before", [P, P])
        ones_f = sb("ones_f", [P, 2])
        ones_col = sb("ones_col", [P, 2], f32r)
        neg_half = sb("neg_half", [P, 2 * TILES])
        dummy_row = sb("dummy_row", [P, TILES])
        g1_rows = sb("g1_rows", [P, P])
        b1_rows = sb("b1_rows", [P, P])
        g1_eps = sb("g1_eps", [P, P])
        b1_tiles = sb("b1_tiles", [P, ROWS])
        fill_rows = sb("fill_rows", [P, FILL * P])
        eps_col = sb("eps_col", [P, 1])
        one_eps = sb("one_eps", [P, 1])
        g2_col = sb("g2_col", [P, 1])
        b2_col = sb("b2_col", [P, 1])
        bg1_col = sb("bg1_col", [P, 1])
        ones_f32 = sb("ones_f32", [P, P])
        ones = sb("ones", [P, P], f32r)
        bg2_rows = sb("bg2_rows", [P, P])
        bg2_hi = sb("bg2_hi", [P, P], f32r)
        bg2_lo = sb("bg2_lo", [P, P])
        bg2_row1 = sb("bg2_row1", [P, P])
        bg2_parts = sb("bg2_parts", [P, ROWS], f32r)
        bf2_col = sb("bf2_col", [P, 1])
        bf1_col = sb("bf1_col", [P, HC])
        bf1_all = sb("bf1_all", [P, HC])
        wg1 = sb("wg1", [P, P])
        wg2 = sb("wg2", [P, P])
        wf1 = sb("wf1", [P, HIDDEN])
        wf1_g = sb("wf1_g", [P, HIDDEN])
        wf1_hi = sb("wf1_hi", [P, HIDDEN], f32r)
        wf1_lo = sb("wf1_lo", [P, HIDDEN], f32r)
        wf2 = sb("wf2", [P, HC, P])
        wf2_hi = sb("wf2_hi", [P, SPLIT, P], f32r)
        wf2_lo = sb("wf2_lo", [P, SPLIT, P], f32r)

        ER = 4
        src_i = [sb(f"src_i{k}", [P, TILES], i32) for k in range(ER)]
        dst_i = [sb(f"dst_i{k}", [P, TILES], i32) for k in range(ER)]
        dst_row_i = [sb(f"dst_row_i{k}", [P, ROWS], i32) for k in range(ER)]
        attr = [sb(f"attr{k}", [P, TILES, P]) for k in range(ER)]
        xs = [sb(f"xs{k}", [P, TILES, P]) for k in range(2)]
        us = sb("us", [P, TILES, P])
        ws = sb("ws", [P, TILES, P])
        attr_b = sb("attr_b", [P, TILES, P])
        pre = [sb(f"pre{k}", [P, TILES, P]) for k in range(2)]
        msg = [sb(f"msg{k}", [P, TILES, P]) for k in range(2)]
        e_raw = sb("e_raw", [P, TILES, 6])
        e_raw2 = sb("e_raw2", [P, TILES, 6])
        e_mv = sb("e_mv", [P, TILES, 2])
        e_mv2 = sb("e_mv2", [P, TILES, 2])
        e_neg = sb("e_neg", [P, TILES])
        e_var = sb("e_var", [P, TILES])
        e_arg = sb("e_arg", [P, TILES])
        e_r = sb("e_r", [P, TILES])
        dst_f = [sb(f"dst_f{k}", [P, TILES]) for k in range(2)]
        dst_row = sb("dst_row", [P, TILES, P])
        same = [sb(f"same{k}", [P, TILES, TILES * P], f32r) for k in range(2)]
        same_before = [sb(f"same_before{k}", [P, TILES, P], f32r) for k in range(2)]
        to_dummy = [sb(f"to_dummy{k}", [P, TILES]) for k in range(2)]
        move = sb("move", [P, TILES])
        where_i = [sb(f"where_i{k}", [P, TILES], i32) for k in range(ER)]
        sums = [sb(f"sums{k}", [P, TILES, P]) for k in range(ER)]

        XR = 4
        xn = [sb(f"xn{k}", [P, TILES, P]) for k in range(XR)]
        tab = [sb(f"tab{k}", [P, TILES, P]) for k in range(2)]
        u = [sb(f"u{k}", [P, TILES, P]) for k in range(2)]
        w = sb("w", [P, TILES, P])
        z = [sb(f"z{k}", [P, TILES, P]) for k in range(2)]
        h = [sb(f"h{k}", [P, TILES, P]) for k in range(2)]
        raw1 = sb("raw1", [P, TILES, 6])
        raw2 = sb("raw2", [P, TILES, 6])
        raw3 = sb("raw3", [P, TILES, 6])
        mv1 = sb("mv1", [P, TILES, 2])
        mv2 = sb("mv2", [P, TILES, 2])
        mv3 = sb("mv3", [P, TILES, 2])
        neg1 = [sb(f"neg1_{k}", [P, TILES]) for k in range(2)]
        neg3 = sb("neg3", [P, TILES])
        var12 = [sb(f"var12_{k}", [P, 2 * TILES]) for k in range(2)]
        r12 = [sb(f"r12_{k}", [P, 2 * TILES]) for k in range(2)]
        var3 = sb("var3", [P, TILES])
        r3 = sb("r3", [P, TILES])
        nb3 = sb("nb3", [P, TILES])
        zT = sb("zT", [P, ROWS])
        aT = sb("aT", [P, ROWS])
        x2 = [sb(f"x2_{k}", [P, TILES, P]) for k in range(2)]
        xn2 = [sb(f"xn2_{k}", [P, TILES, P]) for k in range(2)]
        res = [sb(f"res{k}", [P, TILES, P]) for k in range(XR)]
        xT_hi = sb("xT_hi", [P, ROWS], f32r)
        xT_lo = sb("xT_lo", [P, ROWS], f32r)
        hT = sb("hT", [P, HC, ROWS])
        hT_hi = sb("hT_hi", [P, SPLIT, ROWS], f32r)
        hT_lo = sb("hT_lo", [P, SPLIT, ROWS], f32r)
        yT = sb("yT", [P, ROWS])
        y = [sb(f"y{k}", [P, TILES, P]) for k in range(2)]

        ps_zy = pb("ps_zy", [P, ROWS])
        ps_x = pb("ps_x", [P, ROWS])
        ps_g = pb("ps_g", [P, ROWS])
        ps_a = pb("ps_a", [P, ROWS])
        ps_h = [pb(f"ps_h{k}", [P, ROWS]) for k in range(3)]
        ps_y = pb("ps_y", [P, ROWS])
        ps_sum = [ps_zy, ps_a]
        ps_cnt = [ps_g, ps_x]

        params_in, weights_in, consts_set, ident_ready, prep = sem("params_in"), sem("weights_in"), sem("consts_set"), sem("ident_ready"), sem("prep")
        bf1_folded, parts_ready, fill_ready, table_filled = sem("bf1_folded"), sem("parts_ready"), sem("fill_ready"), sem2("table_filled")
        edge_in, gathered = [sem(f"edge_in_{k}") for k in range(ER)], sem2("gathered")
        es_raw, es_mv, es_neg, es_u, es_raw2, es_mv2 = (sem(n) for n in ("es_raw", "es_mv", "es_neg", "es_u", "es_raw2", "es_mv2"))
        es_var, es_arg, es_r, es_w, es_attr, es_pre, es_msg = (sem(n) for n in ("es_var", "es_arg", "es_r", "es_w", "es_attr", "es_pre", "es_msg"))
        es_dst, es_same, es_dummy, es_cnt, es_move, es_where, es_sum, es_out = (sem(n) for n in ("es_dst", "es_same", "es_dummy", "es_cnt", "es_move", "es_where", "es_sum", "es_out"))
        scattered = sem("scattered")
        x_in, tab_in, stored = [sem(f"x_in_{k}") for k in range(XR)], sem2("tab_in"), sem2("stored")
        n_raw1, n_mv1, n_neg1, n_u, n_raw2, n_mv2 = (sem(n) for n in ("n_raw1", "n_mv1", "n_neg1", "n_u", "n_raw2", "n_mv2"))
        n_var1, n_var2, n_w, n_r12, n_h, n_z = (sem(n) for n in ("n_var1", "n_var2", "n_w", "n_r12", "n_h", "n_z"))
        n_psz, n_zT, n_psa, n_aT, n_psg, n_x2, n_gelu_hi, n_gelu_lo = (sem(n) for n in ("n_psz", "n_zT", "n_psa", "n_aT", "n_psg", "n_x2", "n_gelu_hi", "n_gelu_lo"))
        n_raw3, n_mv3, n_var3, n_r3, n_nb3, n_xn2, n_res = (sem(n) for n in ("n_raw3", "n_mv3", "n_var3", "n_r3", "n_nb3", "n_xn2", "n_res"))
        n_psx, n_hi, n_lo, n_psh, n_gelu, n_used, n_yT, n_psy, n_y = (sem(n) for n in ("n_psx", "n_hi", "n_lo", "n_psh", "n_gelu", "n_used", "n_yT", "n_psy", "n_y"))

        def rows_of(tensor, turn, parts=P):
            start = turn.row(NODES if tensor is not edge_attr else STEPS * ROWS)
            return tensor[bass.ds(start, parts * TILES), :].rearrange("(p j) f -> p j f", j=TILES)

        def every_partition(vector, parts=P):
            return bass.AP(vector.tensor, 0, [[0, parts], [1, vector.shape[0]]])

        def column(vector):
            return vector.rearrange("(p o) -> p o", o=1)

        def step(q, lap=0, low=None):
            return Turn(q, 4, lap, low)

        def group(q, lap=0, low=None):
            return Turn(q, 4, lap, low)

        def parts_of(s):
            return P if s.low < STEPS - 1 else LAST_P

        def edge_turns(eng, period):
            first_lap, last_lap = 1, (STEPS - 1 - 7) // 4

            def steps_of(t, lap=0, low=0):
                return (step(t + k, lap, low + k) if low + k >= 0 and low + k < STEPS else None for k in (7, 6, 5, 4, 3, 0))

            for t in range(-7, 4 * first_lap):
                period(*steps_of(t, 0, t))
            with eng.Fori(first_lap, last_lap) as lap:
                for q in range(4):
                    period(*steps_of(q, lap, 4 * first_lap + q))
            for t in range(4 * last_lap, STEPS):
                period(*steps_of(t, 0, t))

        def node_turns(eng, period):
            first_lap, last_lap = 1, (GROUPS - 6) // 4
            for t in range(-4, 4 * first_lap):
                period(*(group(t + k) if t + k >= 0 else None for k in (4, 3, 2, 1, 0)))
            with eng.Fori(first_lap, last_lap) as lap:
                for q in range(4):
                    period(*(group(q + k, lap, 4 * first_lap + q + k) for k in (4, 3, 2, 1, 0)))
            for t in range(4 * last_lap, GROUPS):
                period(*(group(t + k) if t + k < GROUPS else None for k in (4, 3, 2, 1, 0)))

        block = ctx.enter_context(nc.Block())

        @block.sync
        def _(sp):
            sp.dma_start(b1_rows[:, :], every_partition(b1)).then_inc(params_in, 16)
            sp.dma_start(eps_col[:, :], bass.AP(eps_gin.tensor, 0, [[0, P], [1, 1]])).then_inc(params_in, 16)
            sp.dma_start(g1_rows[:, :], every_partition(g1)).then_inc(params_in, 16)

            def load_weights():
                sp.dma_start(bg2_rows[:, :], every_partition(bg2)).then_inc(weights_in, 16)
                sp.dma_start(bf2_col[:, :], column(bf2)).then_inc(weights_in, 16)
                sp.dma_start(g2_col[:, :], column(g2)).then_inc(weights_in, 16)
                sp.dma_start(b2_col[:, :], column(b2)).then_inc(weights_in, 16)
                sp.dma_start(bg1_col[:, :], column(bg1)).then_inc(weights_in, 16)
                with nc.allow_non_contiguous_dma(reason="one value a partition"):
                    sp.dma_start(bf1_col[:, :], bf1.rearrange("(k p) -> p k", p=P)).then_inc(weights_in, 16)
                sp.dma_start(wg1[:, :], Wg1).then_inc(weights_in, 16)
                sp.dma_start(wg2[:, :], Wg2).then_inc(weights_in, 16)
                sp.dma_start(wf1[:, :], Wf1).then_inc(weights_in, 16)
                sp.dma_start(wf2[:, :, :], Wf2.rearrange("(k p) n -> p k n", p=P)).then_inc(weights_in, 16)

            def load_edges(s):
                k, parts = s.slot(ER), parts_of(s)
                if s.low >= ER:
                    sp.wait_ge(es_pre, s.done(back=ER))
                rows = bass.ds(s.row(STEPS * ROWS), parts * TILES)
                sp.dma_start(src_i[k][0:parts, :], src[rows].rearrange("(p j) -> p j", j=TILES)).then_inc(edge_in[k], 16)
                sp.dma_start(dst_i[k][0:parts, :], dst[rows].rearrange("(p j) -> p j", j=TILES)).then_inc(edge_in[k], 16)
                sp.dma_start(dst_row_i[k][0:parts, 0:parts * TILES],
                             dst[rows].rearrange("(o n) -> o n", o=1).to_broadcast([parts, parts * TILES])).then_inc(edge_in[k], 16)
                sp.dma_start(attr[k][0:parts, :, :], rows_of(edge_attr, s, parts)).then_inc(edge_in[k], 16)

            def fill_table(part):
                if part == 0:
                    sp.wait_ge(fill_ready, 1)
                if part >= 2:
                    sp.wait_ge(table_filled[part % 2], 16 * (part // 2))
                part_rows = TABLE // FILL_PARTS
                there = table[part * part_rows:(part + 1) * part_rows, :].rearrange("(p r) f -> p (r f)", p=P)
                runs = part_rows // P // FILL
                sp.dma_start(there.rearrange("p (r n) -> p r n", r=runs),
                             fill_rows[:, :].rearrange("p (o n) -> p o n", o=1).to_broadcast([P, runs, FILL * P])).then_inc(table_filled[part % 2], 16)

            fill_after = {3: (0, 8), 4: (8, 12), 5: (12, 17), 6: (17, 21), 7: (21, FILL_PARTS)}

            def period(load, gather, stat, message, rows, add):
                if load:
                    load_edges(load)
                    if load.low in fill_after:
                        first_part, last_part = fill_after[load.low]
                        for part in range(first_part, last_part):
                            fill_table(part)
                        if load.low == 4:
                            load_weights()

            edge_turns(sp, period)

            def load_x(g):
                if g.low >= XR:
                    sp.wait_ge(n_res, g.done(back=XR))
                sp.dma_start(xn[g.slot(XR)][:, :, :], rows_of(x, g)).then_inc(x_in[g.slot(XR)], 16)

            def load_tab(g):
                if g.low == 0:
                    sp.wait_ge(scattered, 16 * TILES * STEPS)
                if g.low >= 2:
                    sp.wait_ge(n_z, g.done(back=2))
                sp.dma_start(tab[g.slot(2)][:, :, :], rows_of(table, g)).then_inc(tab_in[g.slot(2)], 16)

            def store(g):
                sp.wait_ge(n_y, g.done())
                if g.low == GROUPS - 1:
                    sp.wait_ge(stored[(GROUPS - 2) % 2], g.after(-1).done_in_slot(2))
                sp.dma_start(rows_of(out, g), y[g.slot(2)][:, :, :]).then_inc(stored[g.slot(2)], 16)

            def period(mean, norm, gin, norm2, mlp):
                if mlp and mlp.low >= 1:
                    store(mlp.after(-1))
                if mean:
                    load_tab(mean)
                    if mean.low + 1 < GROUPS:
                        load_x(mean.after(1))

            load_x(group(0))
            node_turns(sp, period)
            store(group(GROUPS - 1))
            for g in (group(GROUPS - 2), group(GROUPS - 1)):
                sp.wait_ge(stored[g.slot(2)], g.done_in_slot(2))

        @block.gpsimd
        def _(pool):
            nc.gpsimd.memset(ident[:, :], 0.0)
            nc.gpsimd.memset(before[:, :], 1.0)
            nc.gpsimd.memset(ones_f[:, :], 1.0)
            nc.gpsimd.memset(ones_f32[:, :], 1.0)
            nc.gpsimd.memset(neg_half[:, :], -0.5)
            nc.gpsimd.iota(dummy_row[:, :], [[1, TILES]], base=NODES, channel_multiplier=TILES,
                           allow_small_or_imprecise_dtypes=True).then_inc(consts_set, 1)
            pool.wait_ge(consts_set, 1)
            nc.gpsimd.affine_select(out=ident[:, :], in_=ident[:, :], compare_op=ALU.not_equal, fill=1.0,
                                    base=0, pattern=[[-1, P]], channel_multiplier=1)
            nc.gpsimd.affine_select(out=before[:, :], in_=before[:, :], compare_op=ALU.is_gt, fill=0.0,
                                    base=0, pattern=[[1, P]], channel_multiplier=-1).then_inc(ident_ready, 1)

            def gather_x(s):
                k, parts = s.slot(2), parts_of(s)
                pool.wait_ge(edge_in[s.slot(ER)], s.done_in_slot(ER, 64))
                if s.low >= 2:
                    pool.wait_ge(es_raw, s.done(back=2))
                    pool.wait_ge(es_u, s.done(back=2))
                nc.gpsimd.nop(nofuse=True)
                for j in range(TILES):
                    nc.gpsimd.indirect_dma_start(xs[k][0:parts, j, :], None, x,
                                                 bass.IndirectOffsetOnAxis(src_i[s.slot(ER)][0:parts, j:j + 1], 0)).then_inc(gathered[k], 16)

            def scatter_sums(s):
                k, parts = s.slot(ER), parts_of(s)
                pool.wait_ge(es_where, s.done())
                pool.wait_ge(es_out, s.done())
                if s.low == 0:
                    pool.wait_ge(table_filled[0], 16 * ((FILL_PARTS + 1) // 2))
                    pool.wait_ge(table_filled[1], 16 * (FILL_PARTS // 2))
                else:
                    pool.wait_ge(scattered, s.done(16 * TILES, back=1))
                nc.gpsimd.nop(nofuse=True)
                for j in range(TILES):
                    nc.gpsimd.indirect_dma_start(table, bass.IndirectOffsetOnAxis(where_i[k][0:parts, j:j + 1], 0),
                                                 sums[k][0:parts, j, :], None, compute_op=ALU.add).then_inc(scattered, 16)

            def edge_period(load, gather, stat, message, rows, add):
                if add:
                    scatter_sums(add)
                if gather:
                    gather_x(gather)
                if stat:
                    parts = parts_of(stat)
                    pool.wait_ge(es_arg, stat.done())
                    if stat.low >= 1:
                        pool.wait_ge(es_pre, stat.done(back=1))
                    nc.gpsimd.tensor_tensor(e_r[0:parts, :], e_arg[0:parts, :], neg_half[0:parts, 0:TILES], ALU.pow).then_inc(es_r, 1)

            edge_turns(pool, edge_period)

            def low_part(g, c):
                pool.wait_ge(n_gelu_hi, g.done(SPLIT) - (SPLIT - 1 - c))
                if g.low >= 1:
                    pool.wait_ge(n_used, g.done(HC, back=1) - (HC - 1 - DOWN_ORDER.index(c)))
                nc.gpsimd.tensor_tensor(hT_lo[:, c, :], hT[:, c, :], hT_hi[:, c, :].bitcast(f32), ALU.subtract).then_inc(n_gelu_lo, 1)

            def period(mean, norm, gin, norm2, mlp):
                if norm2:
                    g = norm2
                    pool.wait_ge(n_x2, g.done())
                    if g.low >= XR:
                        pool.wait_ge(n_y, g.done(back=XR))
                    nc.gpsimd.tensor_tensor(res[g.slot(XR)][:, :, :], xn[g.slot(XR)][:, :, :], x2[g.slot(2)][:, :, :], ALU.add).then_inc(n_res, 1)
                if norm:
                    g = norm
                    pool.wait_ge(n_var2, g.done())
                    k = g.slot(2)
                    if g.low >= 2:
                        pool.wait_ge(n_z, g.done(back=2))
                        pool.wait_ge(n_h, g.done(back=2))
                    nc.gpsimd.tensor_tensor(r12[k][:, :], var12[k][:, :], neg_half[:, :], ALU.pow).then_inc(n_r12, 1)
                if norm2:
                    g = norm2
                    pool.wait_ge(n_var3, g.done())
                    if g.low >= 1:
                        pool.wait_ge(n_xn2, g.done(back=1))
                    nc.gpsimd.tensor_tensor(r3[:, :], var3[:, :], neg_half[:, 0:TILES], ALU.pow).then_inc(n_r3, 1)
                    pool.wait_ge(n_r3, g.done())
                    nc.gpsimd.tensor_tensor(nb3[:, :], neg3[:, :], r3[:, :], ALU.mult).then_inc(n_nb3, 1)
                    pool.wait_ge(n_nb3, g.done())
                    if g.low >= 2:
                        pool.wait_ge(n_psx, g.done(back=2))
                    nc.gpsimd.nop(nofuse=True)
                    for j in range(TILES):
                        last_xn2 = nc.gpsimd.tensor_scalar(xn2[g.slot(2)][:, j, :], x2[g.slot(2)][:, j, :], r3[:, j:j + 1], nb3[:, j:j + 1], ALU.mult, ALU.add)
                    last_xn2.then_inc(n_xn2, 1)
                if mlp:
                    for c in range(SPLIT):
                        low_part(mlp, c)

            node_turns(pool, period)

        @block.scalar
        def _(act):
            def edge_period(load, gather, stat, message, rows, add):
                if stat:
                    s, k, parts = stat, stat.slot(2), parts_of(stat)
                    act.wait_ge(es_neg, s.done())
                    if s.low >= 1:
                        act.wait_ge(es_w, s.done(back=1))
                    for j in range(TILES):
                        last_u = nc.scalar.activation(us[0:parts, j, :], xs[k][0:parts, j, :], ACT.Relu, bias=e_neg[0:parts, j:j + 1])
                    last_u.then_inc(es_u, 1)
                if rows:
                    s, k, parts = rows, rows.slot(2), parts_of(rows)
                    act.wait_ge(es_sum, s.done())
                    if s.low >= ER:
                        act.wait_ge(scattered, s.done(16 * TILES, back=ER))
                    nc.scalar.activation(sums[s.slot(ER)][0:parts, :, :].rearrange("p j f -> p (j f)"), ps_sum[k][0:parts, :], ACT.Copy).then_inc(es_out, 1)
                if message:
                    s, k, parts = message, message.slot(2), parts_of(message)
                    act.wait_ge(es_pre, s.done())
                    if s.low >= 2:
                        act.wait_ge(es_sum, s.done(back=2))
                    nc.scalar.activation(msg[k][0:parts, :, :], pre[k][0:parts, :, :], ACT.Relu).then_inc(es_msg, 1)

            edge_turns(act, edge_period)

            def mlp_out(g):
                act.wait_ge(n_used, g.done(HC))
                if g.low >= 1:
                    act.wait_ge(n_psy, g.done(back=1))
                nc.scalar.activation(yT[:, :], ps_y[:, :], ACT.Identity, bias=bf2_col[:, 0:1]).then_inc(n_yT, 1)

            def gelu(g, c):
                act.wait_ge(n_psh, g.done(HC) - (HC - 1 - c))
                if g.low >= 1 and c < SPLIT:
                    act.wait_ge(n_gelu_lo, g.done(SPLIT, back=1) - (SPLIT - 1 - c))
                elif g.low >= 1:
                    act.wait_ge(n_used, g.done(HC, back=1) - (HC - 1 - DOWN_ORDER.index(c)))
                nc.scalar.activation(hT[:, c, :], ps_h[c % 3][:, :], ACT.Gelu, bias=bf1_all[:, c:c + 1]).then_inc(n_gelu, 1)
                if c < SPLIT:
                    if g.low >= 1:
                        act.wait_ge(n_used, g.done(HC, back=1) - (HC - 1 - DOWN_ORDER.index(c)))
                    nc.scalar.activation(hT_hi[:, c, :], ps_h[c % 3][:, :], ACT.Gelu, bias=bf1_all[:, c:c + 1]).then_inc(n_gelu_hi, 1)

            def period(mean, norm, gin, norm2, mlp):
                if gin:
                    act.wait_ge(n_psz, gin.done())
                    if gin.low >= 1:
                        act.wait_ge(n_psa, gin.done(back=1))
                    nc.scalar.activation(zT[:, :], ps_zy[:, :], ACT.Copy).then_inc(n_zT, 1)
                if gin:
                    g = gin
                    act.wait_ge(n_r12, g.done())
                    if g.low >= 2:
                        act.wait_ge(n_x2, g.done(back=2))
                    for j in range(TILES):
                        last_h = nc.scalar.activation(h[g.slot(2)][:, j, :], u[g.slot(2)][:, j, :], ACT.Relu, scale=r12[g.slot(2)][:, j:j + 1])
                    last_h.then_inc(n_h, 1)
                if mlp and mlp.low >= 1:
                    mlp_out(mlp.after(-1))
                if mlp:
                    gelu(mlp, 0)
                if gin:
                    g = gin
                    act.wait_ge(n_psa, g.done())
                    if g.low >= 1:
                        act.wait_ge(n_psg, g.done(back=1))
                    nc.scalar.activation(aT[:, :], ps_a[:, :], ACT.Relu, bias=bg1_col[:, 0:1]).then_inc(n_aT, 1)
                if mlp:
                    gelu(mlp, 1)
                    gelu(mlp, 2)
                if mean:
                    g = mean
                    act.wait_ge(n_neg1, g.done())
                    if g.low >= 2:
                        act.wait_ge(n_w, g.done(back=2))
                        act.wait_ge(n_h, g.done(back=2))
                    for j in range(TILES):
                        last_u = nc.scalar.activation(u[g.slot(2)][:, j, :], xn[g.slot(XR)][:, j, :], ACT.Relu, bias=neg1[g.slot(2)][:, j:j + 1])
                    last_u.then_inc(n_u, 1)
                if mlp:
                    gelu(mlp, 3)
                if norm2:
                    g = norm2
                    act.wait_ge(n_psx, g.done())
                    if g.low >= 1:
                        act.wait_ge(n_psh, g.done(HC, back=1))
                    nc.scalar.activation(xT_hi[:, :], ps_x[:, :], ACT.Copy).then_inc(n_hi, 1)

            act.wait_ge(weights_in, 16 * 10)
            act.wait_ge(prep, 6)
            node_turns(act, period)
            mlp_out(group(GROUPS - 1))

        @block.vector
        def _(dve):
            dve.wait_ge(params_in, 16 * 3)
            nc.vector.tensor_scalar(one_eps[:, :], eps_col[:, :], 1.0, None, ALU.add).then_inc(prep, 1)
            dve.wait_ge(prep, 1)
            for r in range(FILL):
                last_fill = nc.vector.tensor_scalar(fill_rows[:, r * P:(r + 1) * P], b1_rows[:, :], one_eps[:, 0:1], None, ALU.mult)
            last_fill.then_inc(fill_ready, 1)
            nc.vector.tensor_scalar(g1_eps[:, :], g1_rows[:, :], one_eps[:, 0:1], None, ALU.mult)
            for j in range(TILES):
                nc.vector.tensor_copy(b1_tiles[:, j * P:(j + 1) * P], b1_rows[:, :])
            dve.wait_ge(ident_ready, 1)
            nc.vector.tensor_copy(ones_col[:, :], ones_f[:, :])

            def edge_period(load, gather, stat, message, rows, add):
                if stat:
                    s, k, parts = stat, stat.slot(2), parts_of(stat)
                    dve.wait_ge(gathered[k], s.done_in_slot(2, 16 * TILES))
                    for j in range(TILES):
                        last_raw = nc.vector.bn_stats(e_raw[0:parts, j, :], xs[k][0:parts, j, :])
                    last_raw.then_inc(es_raw, 1)
                if message:
                    s, k, parts = message, message.slot(2), parts_of(message)
                    dve.wait_ge(edge_in[s.slot(ER)], s.done_in_slot(ER, 64))
                    nc.vector.tensor_copy(dst_f[k][0:parts, :], dst_i[s.slot(ER)][0:parts, :])
                    nc.vector.tensor_copy(dst_row[0:parts, :, 0:parts],
                                          dst_row_i[s.slot(ER)][0:parts, 0:parts * TILES].rearrange("p (q j) -> p j q", j=TILES)).then_inc(es_dst, 1)
                if stat:
                    s, parts = stat, parts_of(stat)
                    dve.wait_ge(es_raw, s.done())
                    nc.vector.nop(nofuse=True)
                    for j in range(TILES):
                        last_mv = nc.vector.bn_aggr(e_mv[0:parts, j, :], e_raw[0:parts, j, :])
                    last_mv.then_inc(es_mv, 1)
                if message:
                    s, k, parts = message, message.slot(2), parts_of(message)
                    dve.wait_ge(es_dst, s.done())
                    nc.vector.tensor_tensor(to_dummy[k][0:parts, :], dummy_row[0:parts, :], dst_f[k][0:parts, :], ALU.subtract).then_inc(es_dummy, 1)
                if stat:
                    s, parts = stat, parts_of(stat)
                    dve.wait_ge(es_mv, s.done())
                    if s.low >= 1:
                        dve.wait_ge(es_u, s.done(back=1))
                    nc.vector.tensor_scalar(e_neg[0:parts, :], e_mv[0:parts, :, 0], -1.0, None, ALU.mult).then_inc(es_neg, 1)
                    nc.vector.tensor_scalar(e_var[0:parts, :], e_mv[0:parts, :, 1], LN_EPS, None, ALU.add).then_inc(es_var, 1)
                if message:
                    s, k, parts = message, message.slot(2), parts_of(message)
                    if s.low >= 2:
                        dve.wait_ge(es_sum, s.done(back=2))
                    for i in range(TILES):
                        nc.vector.scalar_tensor_tensor(out=same_before[k][0:parts, i, 0:parts], in0=dst_row[0:parts, i, 0:parts],
                                                       scalar=dst_f[k][0:parts, i:i + 1], in1=before[0:parts, 0:parts],
                                                       op0=ALU.is_equal, op1=ALU.mult)
                        last_same = nc.vector.tensor_scalar(same[k][0:parts, i, :].rearrange("p (j q) -> p j q", j=TILES)[:, :, 0:parts],
                                                            dst_row[0:parts, :, 0:parts], dst_f[k][0:parts, i:i + 1], None, ALU.is_equal)
                    last_same.then_inc(es_same, 1)
                if rows:
                    s, k, parts = rows, rows.slot(2), parts_of(rows)
                    dve.wait_ge(es_cnt, s.done())
                    dve.wait_ge(es_dummy, s.done())
                    if s.low >= 1:
                        dve.wait_ge(es_where, s.done(back=1))
                    nc.vector.scalar_tensor_tensor(out=move[0:parts, :], in0=ps_cnt[k][0:parts, 0:2 * TILES:2], scalar=1.0, in1=to_dummy[k][0:parts, :],
                                                   op0=ALU.min, op1=ALU.mult).then_inc(es_move, 1)
                if message:
                    s, k, parts = message, message.slot(2), parts_of(message)
                    dve.wait_ge(es_r, s.done())
                    dve.wait_ge(es_w, s.done())
                    dve.wait_ge(es_attr, s.done())
                    if s.low >= 2:
                        dve.wait_ge(es_msg, s.done(back=2))
                    for j in range(TILES):
                        last_pre = nc.vector.scalar_tensor_tensor(out=pre[k][0:parts, j, :], in0=ws[0:parts, j, :], scalar=e_r[0:parts, j:j + 1],
                                                                  in1=attr_b[0:parts, j, :], op0=ALU.mult, op1=ALU.add)
                    last_pre.then_inc(es_pre, 1)
                if rows:
                    s, k, parts = rows, rows.slot(2), parts_of(rows)
                    dve.wait_ge(es_move, s.done())
                    if s.low >= ER:
                        dve.wait_ge(scattered, s.done(16 * TILES, back=ER))
                    nc.vector.tensor_tensor(where_i[s.slot(ER)][0:parts, :], move[0:parts, :], dst_f[k][0:parts, :], ALU.add).then_inc(es_where, 1)
                if stat:
                    s, parts = stat, parts_of(stat)
                    dve.wait_ge(es_u, s.done())
                    for j in range(TILES):
                        last_raw = nc.vector.bn_stats(e_raw2[0:parts, j, :], us[0:parts, j, :])
                    last_raw.then_inc(es_raw2, 1)
                    dve.wait_ge(edge_in[s.slot(ER)], s.done_in_slot(ER, 64))
                    if s.low >= 1:
                        dve.wait_ge(es_pre, s.done(back=1))
                    nc.vector.tensor_tensor(attr_b[0:parts, :, :], attr[s.slot(ER)][0:parts, :, :],
                                            b1_tiles[0:parts, :].rearrange("p (j f) -> p j f", j=TILES), ALU.add).then_inc(es_attr, 1)
                    dve.wait_ge(es_raw2, s.done())
                    nc.vector.nop(nofuse=True)
                    for j in range(TILES):
                        last_mv = nc.vector.bn_aggr(e_mv2[0:parts, j, :], e_raw2[0:parts, j, :])
                    last_mv.then_inc(es_mv2, 1)
                    dve.wait_ge(es_mv2, s.done())
                    dve.wait_ge(es_var, s.done())
                    if s.low >= 1:
                        dve.wait_ge(es_r, s.done(back=1))
                    nc.vector.scalar_tensor_tensor(out=e_arg[0:parts, :], in0=e_var[0:parts, :], scalar=LN_EPS, in1=e_mv2[0:parts, :, 1],
                                                   op0=ALU.mult, op1=ALU.add).then_inc(es_arg, 1)
                    for j in range(TILES):
                        last_w = nc.vector.scalar_tensor_tensor(out=ws[0:parts, j, :], in0=us[0:parts, j, :], scalar=e_mv2[0:parts, j, 0:1],
                                                                in1=g1_rows[0:parts, :], op0=ALU.subtract, op1=ALU.mult)
                    last_w.then_inc(es_w, 1)

            edge_turns(dve, edge_period)

            dve.wait_ge(weights_in, 16 * 10)
            nc.vector.tensor_scalar(wf1_g[:, :], wf1[:, :], g2_col[:, 0:1], None, ALU.mult).then_inc(prep, 1)
            dve.wait_ge(prep, 2)
            nc.vector.tensor_copy(wf1_hi[:, :], wf1_g[:, :]).then_inc(prep, 1)
            dve.wait_ge(prep, 3)
            nc.vector.tensor_tensor(wf1_lo[:, :], wf1_g[:, :], wf1_hi[:, :].bitcast(f32), ALU.subtract)
            for c in range(SPLIT):
                nc.vector.tensor_copy(wf2_hi[:, c, :], wf2[:, c, :])
            nc.vector.tensor_copy(ones[:, :], ones_f32[:, :])
            nc.vector.tensor_copy(bg2_hi[:, :], bg2_rows[:, :]).then_inc(prep, 1)
            dve.wait_ge(prep, 4)
            for c in range(SPLIT):
                nc.vector.tensor_tensor(wf2_lo[:, c, :], wf2[:, c, :], wf2_hi[:, c, :].bitcast(f32), ALU.subtract)
            nc.vector.tensor_tensor(bg2_lo[:, :], bg2_rows[:, :], bg2_hi[:, :].bitcast(f32), ALU.subtract).then_inc(prep, 1)
            dve.wait_ge(prep, 5)
            nc.vector.tensor_scalar(bg2_row1[:, :], bg2_lo[:, :], ident[:, 1:2], None, ALU.mult).then_inc(parts_ready, 1)
            dve.wait_ge(parts_ready, 1)
            for j in range(TILES):
                last_part = nc.vector.scalar_tensor_tensor(out=bg2_parts[:, j * P:(j + 1) * P], in0=bg2_hi[:, :].bitcast(f32), scalar=ident[:, 0:1],
                                                           in1=bg2_row1[:, :], op0=ALU.mult, op1=ALU.add)
            last_part.then_inc(parts_ready, 1)
            dve.wait_ge(bf1_folded, 1)
            nc.vector.tensor_tensor(bf1_all[:, :], ps_y[:, 0:HC], bf1_col[:, :], ALU.add).then_inc(prep, 1)

            def finish(g):
                k = g.slot(2)
                dve.wait_ge(n_psy, g.done())
                dve.wait_ge(n_res, g.done())
                if g.low >= 2:
                    dve.wait_ge(stored[k], g.done_in_slot(2, back=2))
                nc.vector.tensor_tensor(y[k][:, :, :], ps_zy[:, :].rearrange("p (j f) -> p j f", j=TILES), res[g.slot(XR)][:, :, :], ALU.add).then_inc(n_y, 1)

            def period(mean, norm, gin, norm2, mlp):
                if norm:
                    dve.wait_ge(n_u, norm.done())
                    for j in range(TILES):
                        last_raw = nc.vector.bn_stats(raw2[:, j, :], u[norm.slot(2)][:, j, :])
                    last_raw.then_inc(n_raw2, 1)
                if mlp:
                    g = mlp
                    dve.wait_ge(n_hi, g.done())
                    if g.low >= 1:
                        dve.wait_ge(n_psh, g.done(HC, back=1))
                    nc.vector.tensor_tensor(xT_lo[:, :], ps_x[:, :], xT_hi[:, :].bitcast(f32), ALU.subtract).then_inc(n_lo, 1)
                if norm2:
                    g = norm2
                    dve.wait_ge(n_psg, g.done())
                    dve.wait_ge(n_h, g.done())
                    if g.low >= 2:
                        dve.wait_ge(n_xn2, g.done(back=2))
                        dve.wait_ge(n_res, g.done(back=2))
                    nc.vector.tensor_tensor(x2[g.slot(2)][:, :, :], ps_g[:, :].rearrange("p (j f) -> p j f", j=TILES), h[g.slot(2)][:, :, :], ALU.add).then_inc(n_x2, 1)
                if norm:
                    dve.wait_ge(n_raw2, norm.done())
                    nc.vector.nop(nofuse=True)
                    for j in range(TILES):
                        last_mv = nc.vector.bn_aggr(mv2[:, j, :], raw2[:, j, :])
                    last_mv.then_inc(n_mv2, 1)
                if norm:
                    dve.wait_ge(n_mv2, norm.done())
                    dve.wait_ge(n_var1, norm.done())
                    nc.vector.scalar_tensor_tensor(out=var12[norm.slot(2)][:, TILES:2 * TILES], in0=var12[norm.slot(2)][:, 0:TILES], scalar=LN_EPS, in1=mv2[:, :, 1],
                                                   op0=ALU.mult, op1=ALU.add).then_inc(n_var2, 1)
                if norm2:
                    dve.wait_ge(n_x2, norm2.done())
                    for j in range(TILES):
                        last_raw = nc.vector.bn_stats(raw3[:, j, :], x2[norm2.slot(2)][:, j, :])
                    last_raw.then_inc(n_raw3, 1)
                if norm2:
                    dve.wait_ge(n_raw3, norm2.done())
                    nc.vector.nop(nofuse=True)
                    for j in range(TILES):
                        last_mv = nc.vector.bn_aggr(mv3[:, j, :], raw3[:, j, :])
                    last_mv.then_inc(n_mv3, 1)
                if norm2:
                    dve.wait_ge(n_mv3, norm2.done())
                    nc.vector.tensor_scalar(neg3[:, :], mv3[:, :, 0], -1.0, None, ALU.mult)
                    nc.vector.tensor_scalar(var3[:, :], mv3[:, :, 1], LN_EPS, None, ALU.add).then_inc(n_var3, 1)
                if mean:
                    g = mean
                    dve.wait_ge(x_in[g.slot(XR)], g.done_in_slot(XR))
                    for j in range(TILES):
                        last_raw = nc.vector.bn_stats(raw1[:, j, :], xn[g.slot(XR)][:, j, :])
                    last_raw.then_inc(n_raw1, 1)
                if norm:
                    if norm.low >= 1:
                        dve.wait_ge(n_z, norm.done(back=1))
                    for j in range(TILES):
                        last_w = nc.vector.scalar_tensor_tensor(out=w[:, j, :], in0=u[norm.slot(2)][:, j, :], scalar=mv2[:, j, 0:1], in1=g1_eps[:, :],
                                                                op0=ALU.subtract, op1=ALU.mult)
                    last_w.then_inc(n_w, 1)
                if mean:
                    dve.wait_ge(n_raw1, mean.done())
                    nc.vector.nop(nofuse=True)
                    for j in range(TILES):
                        last_mv = nc.vector.bn_aggr(mv1[:, j, :], raw1[:, j, :])
                    last_mv.then_inc(n_mv1, 1)
                if mean:
                    dve.wait_ge(n_mv1, mean.done())
                    k = mean.slot(2)
                    if mean.low >= 2:
                        dve.wait_ge(n_u, mean.done(back=2))
                        dve.wait_ge(n_r12, mean.done(back=2))
                    nc.vector.tensor_scalar(neg1[k][:, :], mv1[:, :, 0], -1.0, None, ALU.mult).then_inc(n_neg1, 1)
                    nc.vector.tensor_scalar(var12[k][:, 0:TILES], mv1[:, :, 1], LN_EPS, None, ALU.add).then_inc(n_var1, 1)
                if norm:
                    g, k = norm, norm.slot(2)
                    dve.wait_ge(n_r12, g.done())
                    dve.wait_ge(n_w, g.done())
                    dve.wait_ge(tab_in[k], g.done_in_slot(2))
                    if g.low >= 2:
                        dve.wait_ge(n_psz, g.done(back=2))
                    for j in range(TILES):
                        last_z = nc.vector.scalar_tensor_tensor(out=z[k][:, j, :], in0=w[:, j, :], scalar=r12[k][:, TILES + j:TILES + j + 1],
                                                                in1=tab[k][:, j, :], op0=ALU.mult, op1=ALU.add)
                    last_z.then_inc(n_z, 1)
                if mlp and mlp.low >= 1:
                    finish(mlp.after(-1))

            node_turns(dve, period)
            finish(group(GROUPS - 1))

        @block.tensor
        def _(pe):
            def edge_period(load, gather, stat, message, rows, add):
                if message:
                    s, k, parts = message, message.slot(2), parts_of(message)
                    pe.wait_ge(es_same, s.done())
                    if s.low >= 2:
                        pe.wait_ge(es_move, s.done(back=2))
                    for j in range(TILES):
                        for i in range(j):
                            nc.tensor.matmul(ps_cnt[k][:, 2 * j:2 * j + 2], same[k][0:parts, i, j * P:(j + 1) * P], ones_col[0:parts, :],
                                             start=(i == 0), stop=False)
                        last_cnt = nc.tensor.matmul(ps_cnt[k][:, 2 * j:2 * j + 2], same_before[k][0:parts, j, :], ones_col[0:parts, :],
                                                    start=(j == 0), stop=True)
                    last_cnt.then_inc(es_cnt, 1)
                    pe.wait_ge(es_msg, s.done())
                    if s.low >= 2:
                        pe.wait_ge(es_out, s.done(back=2))
                    for j in range(TILES):
                        for i in range(TILES):
                            last_sum = nc.tensor.matmul(ps_sum[k][0:parts, j * P:(j + 1) * P], same[k][0:parts, i, j * P:j * P + parts].bitcast(f32),
                                                        msg[k][0:parts, i, :], start=(i == 0), stop=(i == TILES - 1))
                    last_sum.then_inc(es_sum, 1)

            edge_turns(pe, edge_period)

            pe.wait_ge(weights_in, 16 * 10)
            for h in range(HC):
                last_b = nc.tensor.matmul(ps_y[:, h:h + 1], wf1[:, h * P:(h + 1) * P], b2_col[:, 0:1], start=True, stop=True)
            last_b.then_inc(bf1_folded, 1)

            def transposes(bank, rows):
                for j in range(TILES):
                    last_t = nc.tensor.transpose(bank[:, j * P:(j + 1) * P], rows[:, j * P:(j + 1) * P], ident[:, :])
                return last_t

            def flat(tiles):
                return tiles[:, :, :].rearrange("p j f -> p (j f)")

            def up(g, c):
                if c == 3:
                    pe.wait_ge(n_gelu_hi, g.done(SPLIT) - (SPLIT - 1))
                elif g.low >= 1:
                    if c == 0:
                        pe.wait_ge(n_gelu, g.done(HC, back=1))
                    elif c < SPLIT:
                        pe.wait_ge(n_gelu_hi, g.done(SPLIT, back=1) - (SPLIT - 1 - c))
                    else:
                        pe.wait_ge(n_gelu, g.done(HC, back=1) - (HC - 1 - c))
                for n, (part, lhs) in enumerate(((xT_hi, wf1_hi), (xT_hi, wf1_lo), (xT_lo, wf1_hi))):
                    last_h = nc.tensor.matmul(ps_h[c % 3][:, :], lhs[:, c * P:(c + 1) * P], part[:, :], start=(n == 0), stop=(n == 2))
                last_h.then_inc(n_psh, 1)

            def down(g, c):
                first, last = c == DOWN_ORDER[0], c == DOWN_ORDER[-1]
                if first and g.low >= 1:
                    pe.wait_ge(n_yT, g.done(back=1))
                if c < SPLIT:
                    pe.wait_ge(n_gelu_lo, g.done(SPLIT) - (SPLIT - 1 - c))
                    nc.tensor.matmul(ps_y[:, :], wf2_hi[:, c, :], hT_hi[:, c, :], start=first, stop=False)
                    nc.tensor.matmul(ps_y[:, :], wf2_lo[:, c, :], hT_hi[:, c, :], start=False, stop=False)
                    nc.tensor.matmul(ps_y[:, :], wf2_hi[:, c, :], hT_lo[:, c, :], start=False, stop=last).then_inc(n_used, 1)
                else:
                    pe.wait_ge(n_gelu, g.done(HC) - (HC - 1 - c))
                    nc.tensor.matmul(ps_y[:, :], wf2[:, c, :], hT[:, c, :], start=first, stop=last).then_inc(n_used, 1)

            def mlp_rows(g):
                pe.wait_ge(n_yT, g.done())
                if g.low + 3 < GROUPS:
                    pe.wait_ge(n_zT, g.after(3).done())
                else:
                    pe.wait_ge(n_y, g.done(back=1))
                transposes(ps_zy, yT).then_inc(n_psy, 1)

            def period(mean, norm, gin, norm2, mlp):
                if gin:
                    g = gin
                    pe.wait_ge(n_z, g.done())
                    if g.low >= 4:
                        pe.wait_ge(n_y, g.done(back=4))
                    elif g.low >= 1:
                        pe.wait_ge(n_zT, g.done(back=1))
                    transposes(ps_zy, flat(z[g.slot(2)])).then_inc(n_psz, 1)
                if mlp:
                    if mlp.low >= 1:
                        for c in DOWN_ORDER[1:]:
                            down(mlp.after(-1), c)
                    pe.wait_ge(n_lo, mlp.done())
                    up(mlp, 0)
                if gin:
                    g = gin
                    pe.wait_ge(n_zT, g.done())
                    if g.low >= 1:
                        pe.wait_ge(n_aT, g.done(back=1))
                    nc.tensor.matmul(ps_a[:, :], wg1[:, :], zT[:, :], start=True, stop=True).then_inc(n_psa, 1)
                if mlp:
                    up(mlp, 1)
                    if mlp.low >= 1:
                        mlp_rows(mlp.after(-1))
                    up(mlp, 2)
                if gin:
                    g = gin
                    if g.low >= 1:
                        pe.wait_ge(n_x2, g.done(back=1))
                    nc.tensor.matmul(ps_g[:, :], ones[:, :], bg2_parts[:, :], start=True, stop=False)
                    pe.wait_ge(n_aT, g.done())
                    for j in range(TILES):
                        last_g = nc.tensor.matmul(ps_g[:, j * P:(j + 1) * P], aT[:, j * P:(j + 1) * P], wg2[:, :], start=False, stop=(j == TILES - 1))
                    last_g.then_inc(n_psg, 1)
                if mlp:
                    up(mlp, 3)
                    down(mlp, DOWN_ORDER[0])
                if norm2:
                    g = norm2
                    pe.wait_ge(n_xn2, g.done())
                    if g.low >= 1:
                        pe.wait_ge(n_lo, g.done(back=1))
                    transposes(ps_x, flat(xn2[g.slot(2)])).then_inc(n_psx, 1)

            pe.wait_ge(parts_ready, 2)
            node_turns(pe, period)
            for c in DOWN_ORDER[1:]:
                down(group(GROUPS - 1), c)
            mlp_rows(group(GROUPS - 1))


_INS = ['x', 'src', 'dst', 'edge_attr_128', 'L0_gnn_g1', 'L0_gnn_b1', 'L0_gnn_g2', 'L0_gnn_b2', 'L0_gnn_eps_gin', 'L0_gnn_Wg1', 'L0_gnn_bg1',
        'L0_gnn_Wg2', 'L0_gnn_bg2', 'L0_gnn_Wf1', 'L0_gnn_bf1', 'L0_gnn_Wf2', 'L0_gnn_bf2']


def kernel(**inputs):
    import numpy as np
    import concourse.bacc as bacc
    from concourse.bass_utils import run_bass_kernel_spmd

    nc = bacc.Bacc("TRN2", target_bir_lowering=False, num_devices=1)
    arrays, args = {}, []
    for name in _INS:
        a = np.ascontiguousarray(inputs[name])
        if a.ndim == 0:
            a = a.reshape(1)
        arrays[f"{name}_dram"] = a
        args.append(nc.dram_tensor(f"{name}_dram", a.shape, mybir.dt.from_np(a.dtype), kind="ExternalInput").ap())
    args.append(nc.dram_tensor("out_dram", inputs['x'].shape, mybir.dt.float32, kind="ExternalOutput").ap())
    gnn_layer(nc, *args)
    return run_bass_kernel_spmd(nc, [arrays], core_ids=[0]).results[0]["out_dram"]
```
